# Optimizing a Trainium2 kernel written in Bass

```python
import numpy as np
import jax
import jax.numpy as jnp

def _softmax(x, axis=-1):
    return jax.nn.softmax(x, axis=axis)

def _gelu(x):
    return jax.nn.gelu(x, approximate=True)

def _silu(x):
    return jax.nn.silu(x)

def _sigmoid(x):
    return jax.nn.sigmoid(x)

def _layernorm(x, axis=-1, eps=1e-05):
    m = jnp.mean(x, axis=axis, keepdims=True)
    v = jnp.var(x, axis=axis, keepdims=True)
    return (x - m) / jnp.sqrt(v + eps)

def _scatter_add(tgt, idx, src, axis=0):
    return tgt.at[idx].add(src)

def _segment_sum(src, seg, n):
    return jax.ops.segment_sum(src, seg, n)
kernel_name = 'mk_adaln_attn_ffn_d1_seqx_r8_daaafc'

def setup_inputs(seed: int=0):
    np.random.seed(seed)
    _w = jnp.asarray

    def _rec_inputs():
        import jax
        import jax.numpy as jnp
        _rk = jax.random.key(seed)
        x = -0.000125 + 0.9999 * jax.random.normal(jax.random.fold_in(_rk, 1), (128, 32, 512), jnp.float32)
        _lenS = 32 - jax.random.randint(jax.random.fold_in(_rk, 7), (128,), 0, max(1, 32 // 4) + 1, jnp.int32)
        _lenS2 = 32 - jax.random.randint(jax.random.fold_in(_rk, 8), (128,), 0, max(1, 32 // 4) + 1, jnp.int32)
        cond_128 = 0.0061147 + 1.02565 * jax.random.normal(jax.random.fold_in(_rk, 11), (128, 128), jnp.float32)
        fside_S_0 = -0.022604 + 0.987366 * jax.random.normal(jax.random.fold_in(_rk, 12), (32,), jnp.float32)
        return (x, cond_128, fside_S_0)
    x, cond_128, fside_S_0 = _rec_inputs()

    def _L0_cond_setup():
        import jax, jax.numpy as jnp
        import numpy as np
        K = 8
        T = 1.0
        D_EMBD = 128
        IN_C = 32
        OUT_C = 32
        BS = 32
        H = 512
        HID = 128
        key = jax.random.key(seed)
        ks = jax.random.split(key, 10)
        s = lambda fan_in: 1.0 / np.sqrt(fan_in)
        return {'x': jax.random.normal(ks[0], (BS, IN_C, H), dtype=jnp.float32), 'embedding': jax.random.normal(ks[1], (BS, D_EMBD), dtype=jnp.float32), 'W0': jax.random.normal(ks[2], (D_EMBD, HID), dtype=jnp.float32) * s(D_EMBD), 'b0': jnp.zeros((HID,), dtype=jnp.float32), 'W1': jax.random.normal(ks[3], (HID, HID), dtype=jnp.float32) * s(HID), 'b1': jnp.zeros((HID,), dtype=jnp.float32), 'W2': jax.random.normal(ks[4], (HID, K), dtype=jnp.float32) * s(HID), 'b2': jnp.zeros((K,), dtype=jnp.float32), 'weight': jax.random.normal(ks[5], (K, OUT_C, IN_C, 1), dtype=jnp.float32) * s(IN_C), 'bias_k': jax.random.normal(ks[6], (K, OUT_C), dtype=jnp.float32) * 0.1}
    _L0_cond_all = _L0_cond_setup()
    _L0_cond_in = {k: v for k, v in _L0_cond_all.items() if k in ('W0', 'b0', 'W1', 'b1', 'W2', 'b2', 'weight', 'bias_k')}
    del _L0_cond_all

    def _L0_attn_setup():
        import jax, jax.numpy as jnp
        import numpy as np
        HIDDEN = 512
        NHQ = 32
        NHKV = 8
        HEAD_DIM = HIDDEN // NHQ
        THETA = 10000.0

        def _rope(x, theta_base):
            b, h, s, d = x.shape
            inv_freq = 1.0 / theta_base ** (jnp.arange(0, d, 2, dtype=jnp.float32)[:d // 2] / d)
            freqs = jnp.arange(s, dtype=jnp.float32)[:, None] * inv_freq[None, :]
            cos = jnp.cos(freqs).astype(x.dtype)
            sin = jnp.sin(freqs).astype(x.dtype)
            x1, x2 = (x[..., :d // 2], x[..., d // 2:])
            return jnp.concatenate([x1 * cos - x2 * sin, x2 * cos + x1 * sin], axis=-1)
        key = jax.random.key(seed)
        ks = jax.random.split(key, 5)
        std = 1.0 / np.sqrt(HIDDEN)
        x = jax.random.normal(ks[0], (2, 256, HIDDEN), dtype=jnp.float32)
        Wq = jax.random.normal(ks[1], (HIDDEN, HIDDEN), dtype=jnp.float32) * std
        Wk = jax.random.normal(ks[2], (HIDDEN, NHKV * HEAD_DIM), dtype=jnp.float32) * std
        Wv = jax.random.normal(ks[3], (HIDDEN, NHKV * HEAD_DIM), dtype=jnp.float32) * std
        Wo = jax.random.normal(ks[4], (HIDDEN, HIDDEN), dtype=jnp.float32) * std
        return {'x': x, 'Wq': Wq, 'Wk': Wk, 'Wv': Wv, 'Wo': Wo}
    _L0_attn_all = _L0_attn_setup()
    _L0_attn_in = {k: v for k, v in _L0_attn_all.items() if k in ('Wq', 'Wk', 'Wv', 'Wo')}
    del _L0_attn_all

    def _L0_cond2_setup():
        import jax, jax.numpy as jnp
        import numpy as np
        from jax import lax
        N, C_IN, L = (32, 32, 512)
        C_OUT, K, GROUPS = (32, 9, 4)
        C_DIM, PAD, STRIDE = (128, 4, 1)
        key = jax.random.key(seed)
        k1, k2, k3, k4, k5 = jax.random.split(key, 5)
        x = jax.random.normal(k1, (N, C_IN, L), dtype=jnp.float32)
        c = jax.random.normal(k2, (N, C_DIM), dtype=jnp.float32)
        weight = jax.random.normal(k3, (C_OUT, C_IN // GROUPS, K), dtype=jnp.float32)
        c_weight = jax.random.normal(k4, (C_OUT, C_DIM), dtype=jnp.float32)
        bias = jax.random.normal(k5, (C_OUT,), dtype=jnp.float32)
        return {'x': x, 'c': c, 'weight': weight, 'c_weight': c_weight, 'bias': bias}
    _L0_cond2_all = _L0_cond2_setup()
    _L0_cond2_in = {k: v for k, v in _L0_cond2_all.items() if k in ('weight', 'c_weight')}
    del _L0_cond2_all

    def _L0_ffn_setup():
        import jax, jax.numpy as jnp
        import numpy as np
        SCALING = 32.0 / 16.0
        key = jax.random.key(seed)
        ks = jax.random.split(key, 7)
        B, T, D, O, R, E = (4, 256, 512, 512, 16, 8)
        x = jax.random.normal(ks[0], (B, T, D), dtype=jnp.float32)
        base_W = jax.random.normal(ks[1], (O, D), dtype=jnp.float32) * D ** (-0.5)
        base_b = jax.random.normal(ks[2], (O,), dtype=jnp.float32) * 0.01
        router_W = jax.random.normal(ks[3], (2 * E - 1, D), dtype=jnp.float32) * D ** (-0.5)
        router_b = jax.random.normal(ks[4], (2 * E - 1,), dtype=jnp.float32) * 0.01
        A = jax.random.normal(ks[5], (E, R, D), dtype=jnp.float32) * D ** (-0.5)
        Bm = jax.random.normal(ks[6], (E, O, R), dtype=jnp.float32) * R ** (-0.5)
        assigned_idx = 0
        others = [i for i in range(E) if i != assigned_idx]
        expert_map = jnp.array([assigned_idx] * E + others, dtype=jnp.int32)
        return {'x': x, 'base_W': base_W, 'base_b': base_b, 'router_W': router_W, 'router_b': router_b, 'A': A, 'B': Bm, 'expert_map': expert_map}
    _L0_ffn_all = _L0_ffn_setup()
    _L0_ffn_in = {k: v for k, v in _L0_ffn_all.items() if k in ('base_W', 'base_b', 'router_W', 'router_b', 'A', 'B', 'expert_map')}
    del _L0_ffn_all
    return {'x': x, 'cond_128': cond_128, 'fside_S_0': fside_S_0, 'L0_cond_W0': _L0_cond_in['W0'], 'L0_cond_b0': _L0_cond_in['b0'], 'L0_cond_W1': _L0_cond_in['W1'], 'L0_cond_b1': _L0_cond_in['b1'], 'L0_cond_W2': _L0_cond_in['W2'], 'L0_cond_b2': _L0_cond_in['b2'], 'L0_cond_weight': _L0_cond_in['weight'], 'L0_cond_bias_k': _L0_cond_in['bias_k'], 'L0_attn_Wq': _L0_attn_in['Wq'], 'L0_attn_Wk': _L0_attn_in['Wk'], 'L0_attn_Wv': _L0_attn_in['Wv'], 'L0_attn_Wo': _L0_attn_in['Wo'], 'L0_cond2_weight': _L0_cond2_in['weight'], 'L0_cond2_c_weight': _L0_cond2_in['c_weight'], 'L0_ffn_base_W': _L0_ffn_in['base_W'], 'L0_ffn_base_b': _L0_ffn_in['base_b'], 'L0_ffn_router_W': _L0_ffn_in['router_W'], 'L0_ffn_router_b': _L0_ffn_in['router_b'], 'L0_ffn_A': _L0_ffn_in['A'], 'L0_ffn_B': _L0_ffn_in['B'], 'L0_ffn_expert_map': _L0_ffn_in['expert_map']}

def reference(x, cond_128, fside_S_0, L0_cond_W0, L0_cond_b0, L0_cond_W1, L0_cond_b1, L0_cond_W2, L0_cond_b2, L0_cond_weight, L0_cond_bias_k, L0_attn_Wq, L0_attn_Wk, L0_attn_Wv, L0_attn_Wo, L0_cond2_weight, L0_cond2_c_weight, L0_ffn_base_W, L0_ffn_base_b, L0_ffn_router_W, L0_ffn_router_b, L0_ffn_A, L0_ffn_B, L0_ffn_expert_map):
    import jax
    import jax.numpy as jnp

    def _L0_cond_ref(x, embedding, W0, b0, W1, b1, W2, b2, weight, bias_k):
        import jax, jax.numpy as jnp
        import numpy as np
        K = 8
        T = 1.0
        D_EMBD = 128
        IN_C = 32
        OUT_C = 32
        BS = 32
        H = 512
        HID = 128
        h = jax.nn.gelu(embedding @ W0 + b0, approximate=False)
        h = jax.nn.gelu(h @ W1 + b1, approximate=False)
        att = jax.nn.softmax((h @ W2 + b2) / T, axis=-1)
        agg_w = jnp.einsum('bk,koi->boi', att, weight[..., 0])
        agg_b = att @ bias_k
        out = jnp.einsum('boi,bih->boh', agg_w, x) + agg_b[:, :, None]
        return out

    def _L0_attn_ref(x, Wq, Wk, Wv, Wo):
        import jax, jax.numpy as jnp
        import numpy as np
        HIDDEN = 512
        NHQ = 32
        NHKV = 8
        HEAD_DIM = HIDDEN // NHQ
        THETA = 10000.0

        def _rope(x, theta_base):
            b, h, s, d = x.shape
            inv_freq = 1.0 / theta_base ** (jnp.arange(0, d, 2, dtype=jnp.float32)[:d // 2] / d)
            freqs = jnp.arange(s, dtype=jnp.float32)[:, None] * inv_freq[None, :]
            cos = jnp.cos(freqs).astype(x.dtype)
            sin = jnp.sin(freqs).astype(x.dtype)
            x1, x2 = (x[..., :d // 2], x[..., d // 2:])
            return jnp.concatenate([x1 * cos - x2 * sin, x2 * cos + x1 * sin], axis=-1)
        b, s, _ = x.shape
        q_per_kv = NHQ // NHKV
        q = (x @ Wq).reshape(b, s, NHQ, HEAD_DIM).transpose(0, 2, 1, 3)
        k = (x @ Wk).reshape(b, s, NHKV, HEAD_DIM).transpose(0, 2, 1, 3)
        v = (x @ Wv).reshape(b, s, NHKV, HEAD_DIM).transpose(0, 2, 1, 3)
        q = _rope(q, THETA)
        k = _rope(k, THETA)
        qg = q.reshape(b, NHKV, q_per_kv, s, HEAD_DIM)
        scores = jnp.einsum('bkgqd,bkmd->bkgqm', qg, k) / np.sqrt(HEAD_DIM)
        causal = jnp.tril(jnp.ones((s, s), dtype=bool))
        scores = jnp.where(causal, scores, -jnp.inf)
        attn = jax.nn.softmax(scores, axis=-1)
        out = jnp.einsum('bkgqm,bkmd->bkgqd', attn, v)
        out = out.reshape(b, NHQ, s, HEAD_DIM).transpose(0, 2, 1, 3).reshape(b, s, HIDDEN)
        return out @ Wo

    def _L0_cond2_ref(x, c, weight, c_weight, bias):
        import jax, jax.numpy as jnp
        import numpy as np
        from jax import lax
        N, C_IN, L = (32, 32, 512)
        C_OUT, K, GROUPS = (32, 9, 4)
        C_DIM, PAD, STRIDE = (128, 4, 1)
        out = lax.conv_general_dilated(x, weight, window_strides=(STRIDE,), padding=[(PAD, PAD)], dimension_numbers=('NCH', 'OIH', 'NCH'), feature_group_count=GROUPS)
        ctx = jnp.einsum('nd,od->no', c, c_weight)
        out = out + ctx[:, :, None] + bias[None, :, None]
        return out

    def _L0_ffn_ref(x, base_W, base_b, router_W, router_b, A, B, expert_map):
        import jax, jax.numpy as jnp
        import numpy as np
        SCALING = 32.0 / 16.0
        E = A.shape[0]
        base_out = jnp.einsum('btd,od->bto', x, base_W) + base_b
        logits = jnp.einsum('btd,nd->btn', x, router_W) + router_b
        probs = jax.nn.softmax(logits, axis=-1)
        topk_p, topk_i = jax.lax.top_k(probs, E)
        mapped = expert_map[topk_i]
        onehot = (mapped[..., None] == jnp.arange(E)).astype(x.dtype)
        w = jnp.einsum('btk,btke->bte', topk_p, onehot)
        h = jnp.einsum('btd,erd->bter', x, A)
        lora = jnp.einsum('bter,eor->bto', h * w[..., None], B) * SCALING
        return base_out + lora
    x = x + _L0_attn_ref(_L0_cond_ref(x, cond_128, L0_cond_W0, L0_cond_b0, L0_cond_W1, L0_cond_b1, L0_cond_W2, L0_cond_b2, L0_cond_weight, L0_cond_bias_k), L0_attn_Wq, L0_attn_Wk, L0_attn_Wv, L0_attn_Wo)
    x = x + _L0_ffn_ref(_L0_cond2_ref(x, cond_128, L0_cond2_weight, L0_cond2_c_weight, fside_S_0), L0_ffn_base_W, L0_ffn_base_b, L0_ffn_router_W, L0_ffn_router_b, L0_ffn_A, L0_ffn_B, L0_ffn_expert_map)
    return x

_drawn_inputs = setup_inputs


def setup_inputs(seed=0):
    import zlib

    import numpy as np

    out = dict(_drawn_inputs(seed))
    spreads = {'L0_cond_b0': (0.0, 0.8), 'L0_cond_b1': (0.0, 0.711), 'L0_cond_b2': (0.0, 0.633)}
    factors = {'L0_cond_bias_k': 4.358,
     'L0_attn_Wq': 2.687,
     'L0_ffn_base_b': 64.0,
     'L0_ffn_router_b': 47.531}
    for name, (base, spread) in spreads.items():
        noise = np.random.default_rng([zlib.crc32(name.encode()), seed]).standard_normal(out[name].shape)
        drawn = base * np.exp(spread * noise) if base else spread * noise
        out[name] = jnp.asarray(drawn.astype(out[name].dtype))
    for name, factor in factors.items():
        out[name] = (out[name] * factor).astype(out[name].dtype)
    return out
```

```python
from contextlib import ExitStack

import numpy as np

import concourse.bass as bass
from concourse import mybir

F32 = mybir.dt.float32
F32R = mybir.dt.float32r
BF16 = mybir.dt.bfloat16
I32 = mybir.dt.int32
ALU = mybir.AluOpType
ACT = mybir.ActivationFunctionType
AX = mybir.AxisListType

P = 128
B = 128
S = 32
D = 512
NB = P // S
G = B // NB
HD = 16
HALF = HD // 2
NKV = 8
NQ = 4
KC = D // P
PH = 4
TAPS = 9
PAD = 4
SHIFTS = 3
CG = 8
NE = 8
RANK = 16
NR = 2 * NE - 1
NAR = 256
LORA_SCALE = 2.0
NCOND = 8
VW = HD + 1
MASKED = -1e30

C_ID = 0
C_CAUSAL = C_ID + P
C_KV = C_CAUSAL + S
C_SEQ = C_KV + NKV
C_CONV = C_SEQ + NB
C_COS = C_CONV + S
C_SIN = C_COS + HD
C_E = C_SIN + HD
C_N = C_E + NE


def constants():
    c = np.zeros((P, C_N), np.float32)
    r = np.arange(P)
    c[r, C_ID + r] = 1
    m = np.arange(S)
    c[:, C_CAUSAL:C_KV] = np.where(m[None, :] <= (r % S)[:, None], 0, MASKED)
    c[r, C_KV + r // HD] = 1
    c[r, C_SEQ + r // S] = 1
    c[:, C_CONV:C_COS] = (r % S // CG)[:, None] == (m // CG)[None, :]
    inv = (np.float32(1) / np.float32(10000.0) ** (np.arange(0, HD, 2, dtype=np.float32) / np.float32(HD))).astype(np.float32)
    angle = ((r % S).astype(np.float32)[:, None] * inv[None, :]).astype(np.float32)
    c[:, C_COS:C_SIN] = np.tile(np.cos(angle), 2)
    c[:, C_SIN:C_E] = np.concatenate([-np.sin(angle), np.sin(angle)], 1)
    c[:, C_E:C_N] = np.arange(NE)
    return c


def live(u):
    return not isinstance(u, int) or 0 <= u < G


def wait(eng, sem, count):
    if not isinstance(count, int) or count > 0:
        eng.wait_ge(sem, count)


def build(nc, x, cond, fside, cW0, cb0, cW1, cb1, cW2, cb2, cweight, cbias, Wq, Wk, Wv, Wo,
          convw, convc, baseW, baseb, routerW, routerb, loraA, loraB, emap, const, out):
    with ExitStack() as ctx:
        def sb(name, shape, dt=F32):
            return ctx.enter_context(nc.sbuf_tensor(name, shape, dt))

        def sem(name):
            return ctx.enter_context(nc.semaphore(name))

        cst = sb("cst", [P, C_N])
        ident = cst[:, C_ID:C_ID + P]
        kvmask = cst[:, C_KV:C_KV + NKV]
        seqmask = cst[:, C_SEQ:C_SEQ + NB]
        ident16 = sb("ident16", [P, P], BF16)
        causal16 = sb("causal16", [P, D], BF16)
        wqkv_hi = sb("wqkv_hi", [P, KC, D + 2 * P], F32R)
        wqkv_lo = sb("wqkv_lo", [P, KC, D + 2 * P], F32R)
        wo_hi = sb("wo_hi", [P, NQ, D], F32R)
        wo_lo = sb("wo_lo", [P, NQ, D], F32R)
        base_hi = sb("base_hi", [P, PH, D], F32R)
        base_lo = sb("base_lo", [P, PH, D], F32R)
        ar_hi = sb("ar_hi", [P, PH, NAR], F32R)
        ar_lo = sb("ar_lo", [P, PH, NAR], F32R)
        lora_hi = sb("lora_hi", [P, D], F32R)
        lora_lo = sb("lora_lo", [P, D], F32R)
        mixw = sb("mixw", [P, G, NB, S])
        mixb = sb("mixb", [P, B * S])
        convb = sb("convb", [P, B * S])
        convW = sb("convW", [P, SHIFTS, PH, S])
        basebB = sb("basebB", [P, D])
        routerbB = sb("routerbB", [P, NR])
        emapB = sb("emapB", [P, NR], I32)
        emapF = sb("emapF", [P, NR])
        expert = sb("expert", [P, NE, NR])

        raw = sb("raw", [P, 4096 + 3 * D])
        rawq = raw[:, 0:2048].rearrange("p (c n) -> p c n", c=KC)
        rawkv = raw[:, 2048:3072].rearrange("p (c n) -> p c n", c=KC)
        rawA = raw[:, 3072:3584]
        rawB = raw[:, 3584:4096].rearrange("p (j e r) -> p j e r", e=NE, j=PH)
        rawR = raw[:, 4096:4608]
        sx = raw[:, 0:1024]
        pr = raw[:, 1024:2048]
        prT = raw[:, 2048:3072].rearrange("p (k n) -> p k n", k=NKV)
        raw2 = sb("raw2", [P, 4 * D])
        rawo = raw2[:, :].rearrange("p (g n) -> p g n", g=NQ)
        on = raw2[:, 0:D].rearrange("p (b n) -> p b n", b=NB)
        x1 = raw2[:, D:2 * D].rearrange("p (j n) -> p j n", j=PH)
        x1b = raw2[:, 2 * D:3 * D].rearrange("p (j n) -> p j n", j=PH)
        outS = raw2[:, 3 * D:4 * D]
        raw3 = sb("raw3", [P, 4 * D])
        rawbase = raw3[:, :].rearrange("p (j n) -> p j n", j=PH)
        zs = raw3[:, 0:D]
        t1 = raw3[:, D:D + 640]
        t2 = raw3[:, D + 640:D + 1280]

        condS = sb("condS", [P, P])
        condT = sb("condT", [P, P])
        ccS = sb("ccS", [S, P])
        ccT = sb("ccT", [P, S])
        cW0S = sb("cW0S", [P, P])
        cW1S = sb("cW1S", [P, P])
        cW2S = sb("cW2S", [P, NCOND])
        cb0S = sb("cb0S", [P, 1])
        cb1S = sb("cb1S", [P, 1])
        cb2B = sb("cb2B", [P, NCOND])
        cbiasS = sb("cbiasS", [NCOND, S])
        cwS = sb("cwS", [NCOND, S, S])
        fsideB = sb("fsideB", [P, S])
        h1 = sb("h1", [P, P])
        h2 = sb("h2", [P, P])
        att = sb("att", [P, NCOND])
        attE = sb("attE", [P, NCOND])
        attM = sb("attM", [P, 1])
        attZ = sb("attZ", [P, 1])
        attR = sb("attR", [P, 1])
        attT = sb("attT", [NCOND, P])
        aggb = sb("aggb", [P, S])
        ctxb = sb("ctxb", [P, S])
        cvS = sb("cvS", [S, CG * TAPS])
        cvT = sb("cvT", [P, TAPS, S])

        xm = sb("xm", [P, D])
        xr = sb("xr", [P, D])
        ys = sb("ys", [P, D])
        y_hi = sb("y_hi", [P, D], F32R)
        y_lo = sb("y_lo", [P, D], F32R)
        qk = sb("qk", [P, D + P])
        qk_t = sb("qk_t", [P, D + NB * NKV * S])
        qT = qk_t[:, 0:D].rearrange("p (b g q) -> p b g q", b=NB, g=NQ)
        kT = qk_t[:, D:].rearrange("p (b k m) -> p b k m", b=NB, k=NKV)
        cvR = qk_t[0:S, 0:TAPS * P].rearrange("o (k j g i) -> o k j g i", k=TAPS, j=NB, g=S // CG)
        cwR = convb[0:NCOND, :].rearrange("k (o b i) -> k o b i", o=S, b=NB)
        vm = sb("vm", [P, NKV, NB, VW])
        mx = sb("mx", [P, NB * NKV])
        rz = sb("rz", [P, NKV, NB])
        oT_hi = sb("oT_hi", [P, NQ, NB, S], F32R)
        oT_lo = sb("oT_lo", [P, NQ, NB, S], F32R)
        x1ph = sb("x1ph", [P, NB, P + 2])
        z_hi = sb("z_hi", [P, PH, P], F32R)
        z_lo = sb("z_lo", [P, PH, P], F32R)
        arS = sb("arS", [P, NAR])
        lg = sb("lg", [P, NR])
        lgs = sb("lgs", [P, NR])
        ex = sb("ex", [P, NR])
        exZ = sb("exZ", [P, 1])
        exR = sb("exR", [P, 1])
        top = sb("top", [P, 1])
        top2 = sb("top2", [P, 8])
        rest = sb("rest", [P, NR])
        sel = sb("sel", [P, NR])
        selE = sb("selE", [P, NE, NR])
        we = sb("we", [P, NE])
        hw = sb("hw", [P, NE, RANK])
        hwT_hi = sb("hwT_hi", [P, P], F32R)
        hwT_lo = sb("hwT_lo", [P, P], F32R)

        mixb_dram = nc.dram_tensor("mixb_dram", [B, S], F32, kind="Internal").ap()
        convb_dram = nc.dram_tensor("convb_dram", [B, S], F32, kind="Internal").ap()

        bank = [ctx.enter_context(nc.psum_tensor(f"bank{i}", [P, 512], F32)) for i in range(0)]
        ps = ctx.enter_context(nc.psum_tensor("ps", [P, 8, 512], F32))

        names = ("const cond cc fside cW0 cW1 cW2 cb0 cb1 cb2 cbias cw wq wkv wo base A B R convw basebB "
                 "routerbB emap").split()
        ld = {n: sem("ld_" + n) for n in names}
        cT_ps, cT_sb, cc_ps = sem("cT_ps"), sem("cT_sb"), sem("cc_ps")
        h1_ps, h1_sb, h2_ps, h2_sb = sem("h1_ps"), sem("h1_sb"), sem("h2_ps"), sem("h2_sb")
        lg_ps, aM, aE, aZ, att_sb = sem("lg_ps"), sem("aM"), sem("aE"), sem("aZ"), sem("att_sb")
        attT_ps, attT_sb = sem("attT_ps"), sem("attT_sb")
        ctx_ps, ctx_sb, aggb_ps, aggb_sb = sem("ctx_ps"), sem("ctx_sb"), sem("aggb_ps"), sem("aggb_sb")
        ctx_dram, aggb_dram, mixb_in, convb_in = sem("ctx_dram"), sem("aggb_dram"), sem("mixb_in"), sem("convb_in")
        cwR_sb, cvR_sb, cv_ps, cv_sb, convW_sb = sem("cwR_sb"), sem("cvR_sb"), sem("cv_ps"), sem("cv_sb"), sem("convW_sb")
        baseT_ps, arT_ps, loraT_ps = sem("baseT_ps"), sem("arT_ps"), sem("loraT_ps")
        base_hi_sb, base_lo_sb = sem("base_hi_sb"), sem("base_lo_sb")
        ar_hi_sb, ar_lo_sb, lora_hi_sb, lora_lo_sb = sem("ar_hi_sb"), sem("ar_lo_sb"), sem("lora_hi_sb"), sem("lora_lo_sb")
        wqkv_hi_sb, wqkv_lo_sb, wo_hi_sb, wo_lo_sb = sem("wqkv_hi_sb"), sem("wqkv_lo_sb"), sem("wo_hi_sb"), sem("wo_lo_sb")
        mix_ps, mix_sb, masks_sb, emapF_sb, prep_sb = sem("mix_ps"), sem("mix_sb"), sem("masks_sb"), sem("emapF_sb"), sem("prep_sb")

        xm_in, xr_in, out_st = sem("xm_in"), sem("xr_in"), sem("out_st")
        ph_act, ph_dve = sem("ph_act"), sem("ph_dve")
        y_ps, ys_sb, y_hi_sb, y_lo_sb = sem("y_ps"), sem("ys_sb"), sem("y_hi_sb"), sem("y_lo_sb")
        qkv_ps, rope_t, qk_sb, vm_sb = sem("qkv_ps"), sem("rope_t"), sem("qk_sb"), sem("vm_sb")
        qT_ps, qT_sb, kT_sb = sem("qT_ps"), sem("qT_sb"), sem("kT_sb")
        s_ps, mx_sb, sx_sb, p_sb = sem("s_ps"), sem("mx_sb"), sem("sx_sb"), sem("p_sb")
        pT_ps, pT_sb, o_ps, rz_sb, on_sb = sem("pT_ps"), sem("pT_sb"), sem("o_ps"), sem("rz_sb"), sem("on_sb")
        oT_ps, oT_hi_sb, oT_lo_sb = sem("oT_ps"), sem("oT_hi_sb"), sem("oT_lo_sb")
        wo_ps, x1_sb, x1b_sb = sem("wo_ps"), sem("x1_sb"), sem("x1b_sb")
        z_ps, zs_sb, z_hi_sb, z_lo_sb = sem("z_ps"), sem("zs_sb"), sem("z_hi_sb"), sem("z_lo_sb")
        ar_ps, ar_sb, lg_sb, top_sb, lgs_sb = sem("ar_ps"), sem("ar_sb"), sem("lg_sb"), sem("top_sb"), sem("lgs_sb")
        ex_sb, top2_sb, rest_sb, sel_sb, selE_sb = sem("ex_sb"), sem("top2_sb"), sem("rest_sb"), sem("sel_sb"), sem("selE_sb")
        we_sb, hw_sb, hwT_ps, hwT_hi_sb, hwT_lo_sb = sem("we_sb"), sem("hw_sb"), sem("hwT_ps"), sem("hwT_hi_sb"), sem("hwT_lo_sb")
        ffn_ps, out_sb = sem("ffn_ps"), sem("out_sb")

        x_g = x.rearrange("(g b) s d -> g (b s) d", b=NB)
        out_g = out.rearrange("(g b) s d -> g (b s) d", b=NB)

        def group(ap, u):
            return ap[bass.ds(u, 1), :, :].rearrange("a p n -> (a p) n")

        def iterate(eng, steps):
            for t in range(-1, 3):
                steps(t)
            with eng.Fori(3, G - 1) as t:
                steps(t)
            for t in range(G - 1, G + 2):
                steps(t)

        def by_phase(copy, phases):
            for j in phases:
                for b in range(NB):
                    last = copy(x1ph[S * j:S * (j + 1), b, 1:P + 1], x1[S * b:S * (b + 1), j, :])
            return last

        block = ctx.enter_context(nc.Block())

        @block.sync
        def _(sp):
            sp.dma_start(condS[:, :], cond).then_inc(ld["cond"], 16)
            sp.dma_start(cst[:, :], const).then_inc(ld["const"], 16)
            sp.dma_start(cW0S[:, :], cW0).then_inc(ld["cW0"], 16)
            sp.dma_start(cb0S[:, :], cb0.rearrange("(p a) -> p a", a=1)).then_inc(ld["cb0"], 16)
            sp.dma_start(cW1S[:, :], cW1).then_inc(ld["cW1"], 16)
            sp.dma_start(cb1S[:, :], cb1.rearrange("(p a) -> p a", a=1)).then_inc(ld["cb1"], 16)
            sp.dma_start(cW2S[:, :], cW2).then_inc(ld["cW2"], 16)
            sp.dma_start(cb2B[:, :], cb2.partition_broadcast(P)).then_inc(ld["cb2"], 16)
            sp.dma_start(cbiasS[:, :], cbias).then_inc(ld["cbias"], 16)
            sp.dma_start(cwS[:, :, :], cweight.rearrange("k o i a -> k o (i a)")).then_inc(ld["cw"], 16)
            sp.dma_start(xm[:, :], group(x_g, 0)).then_inc(xm_in, 16)
            sp.dma_start(rawq, Wq.rearrange("(c p) n -> p c n", p=P)).then_inc(ld["wq"], 16)
            sp.dma_start(rawkv[:, :, 0:P], Wk.rearrange("(c p) n -> p c n", p=P)).then_inc(ld["wkv"], 16)
            sp.dma_start(rawkv[:, :, P:2 * P], Wv.rearrange("(c p) n -> p c n", p=P)).then_inc(ld["wkv"], 16)
            sp.wait_ge(ctx_sb, 1)
            sp.dma_start(convb_dram, ctxb[:, :]).then_inc(ctx_dram, 16)
            sp.wait_ge(aggb_sb, 1)
            sp.dma_start(mixb_dram, aggb[:, :]).then_inc(aggb_dram, 16)
            sp.wait_ge(aggb_dram, 16)
            sp.dma_start(mixb[:, :], mixb_dram.rearrange("b s -> (b s)").partition_broadcast(P)).then_inc(mixb_in, 16)
            sp.wait_ge(mix_ps, S // NB)
            sp.wait_ge(ctx_dram, 16)
            sp.dma_start(convb[:, :], convb_dram.rearrange("b s -> (b s)").partition_broadcast(P)).then_inc(convb_in, 16)

            def steps(t):
                if live(t - 1):
                    wait(sp, x1_sb, t - 1)
                    sp.dma_start(xr[:, :], group(x_g, t - 1)).then_inc(xr_in, 16)
                if live(t - 2):
                    wait(sp, out_sb, t - 1)
                    sp.dma_start(group(out_g, t - 2), outS).then_inc(out_st, 16)
                if live(t + 1) and live(t + 2):
                    wait(sp, y_ps, t + 2)
                    sp.dma_start(xm[:, :], group(x_g, t + 2)).then_inc(xm_in, 16)

            for t in range(-1, 3):
                steps(t)
            with sp.Fori(3, G - 2) as t:
                steps(t)
            for t in range(G - 2, G + 2):
                steps(t)
            sp.wait_ge(out_st, 16 * G)

        @block.tensor
        def _(pe):
            mm = nc.tensor.matmul

            def product(dst, left, right):
                n = 0
                for c in range(len(left)):
                    (lh, ll), (rh, rl) = left[c], right[c]
                    for a, b in ((lh, rh), (lh, rl), (ll, rh)):
                        last = mm(dst, a, b, start=(n == 0), stop=(n == 3 * len(left) - 1))
                        n += 1
                return last

            pe.wait_ge(ld["const"], 16)
            pe.wait_ge(ld["cond"], 16)
            nc.tensor.transpose(ps[:, 0, 0:P], condS[:, :], ident).then_inc(cT_ps, 1)
            pe.wait_ge(ld["cc"], 16)
            nc.tensor.transpose(ps[:, 3, 0:S], ccS[:, :], cst[0:S, C_ID:C_ID + S]).then_inc(cc_ps, 1)
            pe.wait_ge(cT_sb, 1)
            pe.wait_ge(ld["cW0"], 16)
            mm(ps[:, 1, 0:P], cW0S[:, :], condT[:, :], start=True, stop=True).then_inc(h1_ps, 1)
            pe.wait_ge(cT_sb, 2)
            mm(ps[:, 2, 0:S], condT[:, :], ccT[:, :], start=True, stop=True).then_inc(ctx_ps, 1)
            pe.wait_ge(ld["cW1"], 16)
            pe.wait_ge(h1_sb, 1)
            mm(ps[:, 1, 0:P], cW1S[:, :], h1[:, :], start=True, stop=True).then_inc(h2_ps, 1)
            pe.wait_ge(ld["cW2"], 16)
            pe.wait_ge(h2_sb, 1)
            mm(ps[:, 1, 0:NCOND], h2[:, :], cW2S[:, :], start=True, stop=True).then_inc(lg_ps, 1)
            pe.wait_ge(cvR_sb, 1)
            for k in range(TAPS):
                last = nc.tensor.transpose(ps[:, 3, k * S:(k + 1) * S],
                                           cvR[:, k, :, :, :].rearrange("o j g i -> o (j g i)"),
                                           cst[0:S, C_ID:C_ID + S])
            last.then_inc(cv_ps, 1)
            pe.wait_ge(ld["base"], 16)
            for j in range(PH):
                for jo in range(PH):
                    last = nc.tensor.transpose(ps[:, 4 + j, jo * P:(jo + 1) * P],
                                               rawbase[:, jo, :].rearrange("o (p j) -> o j p", j=PH)[:, j, :],
                                               ident)
                last.then_inc(baseT_ps, 1)
            pe.wait_ge(att_sb, 1)
            nc.tensor.transpose(ps[0:NCOND, 0, 0:P], att[:, :], ident).then_inc(attT_ps, 1)
            pe.wait_ge(attT_sb, 1)
            pe.wait_ge(ld["cbias"], 16)
            pe.wait_ge(ctx_sb, 1)
            mm(ps[:, 2, 0:S], attT[:, :], cbiasS[:, :], start=True, stop=True).then_inc(aggb_ps, 1)
            pe.wait_ge(cwR_sb, 1)
            for n in range(S // NB):
                if n == 1:
                    pe.wait_ge(att_sb, 1)
                if n >= 2:
                    pe.wait_ge(mix_sb, n - 1)
                for i in range(NB):
                    last = mm(ps[:, n % 2, i * P:(i + 1) * P],
                              cwR[:, n * NB + i, :, :].rearrange("k b i -> k (b i)"), attT[:, :],
                              start=True, stop=True)
                last.then_inc(mix_ps, 1)
            pe.wait_ge(ld["A"], 16)
            pe.wait_ge(ld["R"], 16)
            pe.wait_ge(base_lo_sb, 2)
            pe.wait_ge(base_hi_sb, 2)
            for j in range(PH):
                at = ps[:, 4 + j // 2, :].rearrange("p (c n) -> p c n", c=2)[:, j % 2, :]
                nc.tensor.transpose(at[:, 0:P], rawA.rearrange("o (p j) -> o j p", j=PH)[:, j, :], ident)
                last = nc.tensor.transpose(at[:, P:P + NR],
                                           rawR[0:NR, :].rearrange("o (p j) -> o j p", j=PH)[:, j, :],
                                           cst[0:NR, C_ID:C_ID + NR])
                if j % 2:
                    last.then_inc(arT_ps, 1)
            pe.wait_ge(ld["B"], 16 * PH)
            pe.wait_ge(base_lo_sb, 3)
            pe.wait_ge(base_hi_sb, 3)
            for j in range(PH):
                last = nc.tensor.transpose(ps[:, 6, j * P:(j + 1) * P], rawB[:, j, :, :].rearrange("p e r -> p (e r)"), ident)
            last.then_inc(loraT_ps, 1)
            pe.wait_ge(mix_sb, S // NB)
            pe.wait_ge(prep_sb, 1)

            def mix(u):
                pe.wait_ge(xm_in, 16 * (u + 1))
                wait(pe, out_sb, u - 2)
                for c in range(KC):
                    last = mm(ps[:, 6, c * P:(c + 1) * P], xm[:, c * P:(c + 1) * P],
                              mixw[:, bass.ds(u, 1), :, :].rearrange("p a b o -> p (a b o)"),
                              start=True, stop=True)
                last.then_inc(y_ps, 1)

            def qkv(t):
                pe.wait_ge(y_hi_sb, t + 1)
                pe.wait_ge(y_lo_sb, t + 1)
                wait(pe, sx_sb, t)
                y = [(y_hi[:, c * P:(c + 1) * P], y_lo[:, c * P:(c + 1) * P]) for c in range(KC)]
                product(ps[:, 0, :], y, [(wqkv_hi[:, c, 0:D], wqkv_lo[:, c, 0:D]) for c in range(KC)])
                product(ps[:, 1, 0:2 * P], y,
                        [(wqkv_hi[:, c, D:D + 2 * P], wqkv_lo[:, c, D:D + 2 * P]) for c in range(KC)]
                        ).then_inc(qkv_ps, 1)

            def project(u):
                pe.wait_ge(oT_hi_sb, u + 1)
                pe.wait_ge(oT_lo_sb, u + 1)
                o = [tuple(w[:, g, :, :].rearrange("p b q -> p (b q)") for w in (oT_hi, oT_lo)) for g in range(NQ)]
                product(ps[:, 4, :], o, [(wo_hi[:, g, :], wo_lo[:, g, :]) for g in range(NQ)]).then_inc(wo_ps, 1)

            def transpose_qk(t):
                pe.wait_ge(qk_sb, t + 1)
                for g in range(NQ):
                    nc.tensor.transpose(ps[:, 2, g * P:(g + 1) * P], qk[:, g * P:(g + 1) * P], ident)
                nc.tensor.transpose(ps[:, 3, 0:P], qk[:, D:D + P], ident).then_inc(qT_ps, 1)

            def transpose_hw(u):
                pe.wait_ge(hw_sb, u + 1)
                nc.tensor.transpose(ps[:, 7, 0:P], hw[:, :, :].rearrange("p e r -> p (e r)"), ident).then_inc(hwT_ps, 1)

            def base(u):
                z = [(z_hi[:, j, :], z_lo[:, j, :]) for j in range(PH)]
                n = 0
                for j in range(PH):
                    for a, b in ((z_hi, base_hi), (z_hi, base_lo), (z_lo, base_hi)):
                        mm(ps[:, 6, :], a[:, j, :], b[:, j, :], start=(n == 0), stop=False)
                        n += 1

            def scores(t):
                pe.wait_ge(qT_sb, t + 1)
                pe.wait_ge(kT_sb, t + 1)
                pe.wait_ge(vm_sb, t + 1)
                for h in range(2):
                    mm(ps[:, h, :], ident16[:, :], causal16[:, :], start=True, stop=False)
                    for b in (2 * h, 2 * h + 1):
                        last = mm(ps[:, h, (b % 2) * 256:(b % 2) * 256 + 256], qT[:, b, :, :].rearrange("p g q -> p (g q)"),
                                  kT[:, b, :, :].rearrange("p k m -> p (k m)"), start=False, stop=(b % 2 == 1))
                last.then_inc(s_ps, 1)

            def lora(u):
                pe.wait_ge(hwT_hi_sb, u + 1)
                pe.wait_ge(hwT_lo_sb, u + 1)
                mm(ps[:, 6, :], hwT_hi[:, :], lora_hi[:, :], start=False, stop=False)
                mm(ps[:, 6, :], hwT_hi[:, :], lora_lo[:, :], start=False, stop=False)
                mm(ps[:, 6, :], hwT_lo[:, :], lora_hi[:, :], start=False, stop=True).then_inc(ffn_ps, 1)

            def conv(u):
                pe.wait_ge(ph_act, u + 1)
                pe.wait_ge(ph_dve, u + 1)
                zo = ps[:, 5, :].rearrange("p (j t) -> p j t", j=PH)
                for b in range(NB):
                    for s in range(SHIFTS):
                        last = mm(zo[:, :, b * S:(b + 1) * S], x1ph[:, b, s:s + P],
                                  convW[:, s, :, :], start=(s == 0), stop=(s == SHIFTS - 1))
                last.then_inc(z_ps, 1)

            def transpose_p(t):
                pe.wait_ge(p_sb, t + 1)
                for k in range(NKV):
                    last = nc.tensor.transpose(ps[:, 2 + k // 4, (k % 4) * P:(k % 4 + 1) * P], pr[:, k * P:(k + 1) * P], ident)
                    if k % 4 == 3:
                        last.then_inc(pT_ps, 1)

            def values(t):
                wait(pe, zs_sb, t)
                for k in range(NKV):
                    if k % 4 == 0:
                        pe.wait_ge(pT_sb, 2 * t + 1 + k // 4)
                    last = mm(ps[:, 4 + k // 4, (k % 4) * NB * VW:(k % 4 + 1) * NB * VW], prT[:, k, :],
                              vm[:, k, :, :].rearrange("p b c -> p (b c)"), start=True, stop=True)
                last.then_inc(o_ps, 1)

            def heads(u):
                pe.wait_ge(z_hi_sb, u + 1)
                pe.wait_ge(z_lo_sb, u + 1)
                z = [(z_hi[:, j, :], z_lo[:, j, :]) for j in range(PH)]
                product(ps[:, 7, 0:NAR], z, [(ar_hi[:, j, :], ar_lo[:, j, :]) for j in range(PH)]).then_inc(ar_ps, 1)

            def transpose_o(t):
                pe.wait_ge(on_sb, t + 1)
                wait(pe, ys_sb, t + 2 if live(t + 1) else 0)
                for b in range(NB):
                    last = nc.tensor.transpose(ps[:, 6, b * P:(b + 1) * P], on[:, b, :], ident)
                last.then_inc(oT_ps, 1)

            def steps(t):
                if live(t):
                    qkv(t)
                if live(t - 1):
                    project(t - 1)
                if live(t):
                    transpose_qk(t)
                if live(t - 2):
                    transpose_hw(t - 2)
                    base(t - 2)
                if live(t):
                    scores(t)
                if live(t - 2):
                    lora(t - 2)
                if live(t - 1):
                    conv(t - 1)
                if live(t):
                    transpose_p(t)
                if live(t + 1):
                    mix(t + 1)
                if live(t):
                    values(t)
                if live(t - 1):
                    heads(t - 1)
                if live(t):
                    transpose_o(t)

            iterate(pe, steps)

        @block.scalar
        def _(act):
            act.dma_start(ccS[:, :], convc).then_inc(ld["cc"], 16)
            act.dma_start(fsideB[:, :], fside.partition_broadcast(P)).then_inc(ld["fside"], 16)
            act.dma_start(cvS[:, :], convw.rearrange("o i k -> o (i k)")).then_inc(ld["convw"], 16)
            act.dma_start(rawbase, baseW.rearrange("(p j) l -> p j l", j=PH)).then_inc(ld["base"], 16)
            for k in range(NKV):
                act.dma_start(rawo[HD * k:HD * (k + 1), :, :],
                              Wo.rearrange("(k g d) n -> k d g n", k=NKV, g=NQ)[k]).then_inc(ld["wo"], 16)
            act.dma_start(rawA, loraA.rearrange("e r l -> (e r) l")).then_inc(ld["A"], 16)
            act.dma_start(rawR[0:NR, :], routerW).then_inc(ld["R"], 16)
            for j in range(PH):
                act.dma_start(rawB[:, j, :, :], loraB.rearrange("e (p j) r -> j p e r", j=PH)[j]).then_inc(ld["B"], 16)
            act.dma_start(emapB[:, :], emap.partition_broadcast(P)).then_inc(ld["emap"], 16)
            act.dma_start(routerbB[:, :], routerb.partition_broadcast(P)).then_inc(ld["routerbB"], 16)
            act.dma_start(basebB[:, :], baseb.partition_broadcast(P)).then_inc(ld["basebB"], 16)

            def copy(dst, src):
                return nc.scalar.activation(dst, src, ACT.Copy)

            act.wait_ge(h1_ps, 1)
            act.wait_ge(ld["cb0"], 16)
            nc.scalar.activation(h1[:, :], ps[:, 1, 0:P], ACT.Gelu, bias=cb0S[:, :]).then_inc(h1_sb, 1)
            act.wait_ge(h2_ps, 1)
            act.wait_ge(ld["cb1"], 16)
            nc.scalar.activation(h2[:, :], ps[:, 1, 0:P], ACT.Gelu, bias=cb1S[:, :]).then_inc(h2_sb, 1)
            act.wait_ge(aM, 1)
            nc.scalar.activation(attE[:, :], att[:, :], ACT.Exp, bias=attM[:, :], accum_out=attZ[:, :]).then_inc(aE, 1)
            act.wait_ge(ld["wq"], 16)
            for c in range(KC):
                copy(wqkv_hi[:, c, 0:D].rearrange("p (g k d) -> p g k d", g=NQ, k=NKV),
                     rawq[:, c, :].rearrange("p (k g d) -> p g k d", k=NKV, g=NQ)).then_inc(wqkv_hi_sb, 1)
            act.wait_ge(ld["wkv"], 32)
            copy(wqkv_hi[:, :, D:D + 2 * P], rawkv).then_inc(wqkv_hi_sb, 1)
            act.wait_ge(ld["wo"], 16 * NKV)
            for g in range(NQ):
                copy(wo_hi[:, g, :].rearrange("p (j n) -> p j n", j=PH),
                     rawo[:, g, :].rearrange("p (n j) -> p j n", j=PH)).then_inc(wo_hi_sb, 1)
            for j in range(PH):
                act.wait_ge(baseT_ps, j + 1)
                copy(base_hi[:, j, :], ps[:, 4 + j, :]).then_inc(base_hi_sb, 1)
            for h in range(2):
                act.wait_ge(arT_ps, h + 1)
                copy(ar_hi[:, 2 * h:2 * h + 2, 0:P + NR],
                     ps[:, 4 + h, :].rearrange("p (c n) -> p c n", c=2)[:, :, 0:P + NR]).then_inc(ar_hi_sb, 1)
            act.wait_ge(loraT_ps, 1)
            copy(lora_hi[:, :], ps[:, 6, :]).then_inc(lora_hi_sb, 1)

            def steps(t):
                if live(t - 1):
                    act.wait_ge(oT_ps, t)
                    copy(oT_hi[:, :, :, :], ps[:, 6, :].rearrange("p (b g q) -> p g b q", b=NB, g=NQ)).then_inc(oT_hi_sb, 1)
                if live(t - 2):
                    act.wait_ge(lgs_sb, t - 1)
                    nc.scalar.activation(ex[:, :], lgs[:, :], ACT.Exp).then_inc(ex_sb, 1)
                if live(t):
                    act.wait_ge(qT_ps, t + 1)
                    copy(qT, ps[:, 2, :].rearrange("p (g b q) -> p b g q", g=NQ, b=NB)).then_inc(qT_sb, 1)
                if live(t - 1):
                    act.wait_ge(x1_sb, t)
                    by_phase(copy, (1, 3)).then_inc(ph_act, 1)
                if live(t - 2):
                    act.wait_ge(hwT_ps, t - 1)
                    copy(hwT_hi[:, :], ps[:, 7, 0:P]).then_inc(hwT_hi_sb, 1)
                if live(t):
                    act.wait_ge(sx_sb, t + 1)
                    nc.scalar.activation(pr.rearrange("p (k b m) -> p b k m", k=NKV, b=NB),
                                         sx.rearrange("p (b k m) -> p b k m", b=NB, k=NKV), ACT.Exp, scale=HD ** -0.5).then_inc(p_sb, 1)
                if live(t - 1):
                    act.wait_ge(zs_sb, t)
                    copy(z_hi[:, :, :].rearrange("p j n -> p (j n)"), zs).then_inc(z_hi_sb, 1)
                if live(t):
                    for h in range(2):
                        act.wait_ge(pT_ps, 2 * t + 1 + h)
                        copy(prT[:, 4 * h:4 * h + 4, :].rearrange("p k n -> p (k n)"), ps[:, 2 + h, :]).then_inc(pT_sb, 1)
                if live(t + 1):
                    act.wait_ge(ys_sb, t + 2)
                    copy(y_hi[:, :], ys[:, :]).then_inc(y_hi_sb, 1)
                if live(t - 1):
                    act.wait_ge(ar_ps, t)
                    copy(arS[:, :], ps[:, 7, 0:NAR]).then_inc(ar_sb, 1)

            iterate(act, steps)

        @block.gpsimd
        def _(pool):
            def steps(t):
                if live(t - 1):
                    pool.wait_ge(zs_sb, t)
                    pool.wait_ge(z_hi_sb, t)
                    nc.gpsimd.tensor_tensor(z_lo[:, :, :].rearrange("p j n -> p (j n)"), zs,
                                            z_hi[:, :, :].rearrange("p j n -> p (j n)").bitcast(F32),
                                            ALU.subtract).then_inc(z_lo_sb, 1)
                if live(t + 1):
                    pool.wait_ge(y_hi_sb, t + 2)
                    nc.gpsimd.tensor_tensor(y_lo[:, :], ys[:, :], y_hi[:, :].bitcast(F32),
                                            ALU.subtract).then_inc(y_lo_sb, 1)
                if live(t - 1):
                    pool.wait_ge(x1_sb, t)
                    pool.wait_ge(ld["basebB"], 16)
                    wait(pool, out_sb, t - 1)
                    nc.gpsimd.tensor_tensor(x1b, x1, basebB[:, :].rearrange("p (n j) -> p j n", j=PH),
                                            ALU.add).then_inc(x1b_sb, 1)

            iterate(pool, steps)

        @block.vector
        def _(dve):
            v = nc.vector

            def minus(dst, value, hi):
                return v.tensor_tensor(dst, value, hi.bitcast(F32), ALU.subtract)

            dve.wait_ge(cT_ps, 1)
            v.tensor_copy(condT[:, :], ps[:, 0, 0:P]).then_inc(cT_sb, 1)
            dve.wait_ge(cc_ps, 1)
            v.tensor_copy(ccT[:, :], ps[:, 3, 0:S]).then_inc(cT_sb, 1)
            dve.wait_ge(ld["cw"], 16)
            v.tensor_copy(cwR, cwS[:, :, :].unsqueeze(2).broadcast_to([NCOND, S, NB, S])).then_inc(cwR_sb, 1)
            dve.wait_ge(ctx_ps, 1)
            dve.wait_ge(ld["fside"], 16)
            v.tensor_tensor(ctxb[:, :], ps[:, 2, 0:S], fsideB[:, :], ALU.add).then_inc(ctx_sb, 1)
            dve.wait_ge(ld["convw"], 16)
            for j in range(NB):
                for g in range(S // CG):
                    last = v.tensor_copy(cvR[:, :, j, g, :], cvS[:, :].rearrange("o (i k) -> o k i", i=CG))
            last.then_inc(cvR_sb, 1)
            dve.wait_ge(lg_ps, 1)
            dve.wait_ge(ld["cb2"], 16)
            v.tensor_tensor(att[:, :], ps[:, 1, 0:NCOND], cb2B[:, :], ALU.add).then_inc(aZ, 1)
            dve.wait_ge(aZ, 1)
            v.tensor_reduce(attM[:, :], att[:, :], AX.X, ALU.max, negate=True).then_inc(aM, 1)
            dve.wait_ge(aE, 1)
            v.reciprocal(attR[:, :], attZ[:, :]).then_inc(aZ, 1)
            dve.wait_ge(aZ, 2)
            v.tensor_scalar(att[:, :], attE[:, :], attR[:, :], None, ALU.mult).then_inc(att_sb, 1)
            v.memset(ar_hi[:, :, P + NR:NAR].bitcast(F32), 0.0)
            v.memset(ar_lo[:, :, P + NR:NAR].bitcast(F32), 0.0)
            v.memset(x1ph[:, :, :], 0.0)
            v.memset(convW[:, :, :, :], 0.0).then_inc(convW_sb, 1)
            dve.wait_ge(attT_ps, 1)
            v.tensor_copy(attT[:, :], ps[0:NCOND, 0, 0:P]).then_inc(attT_sb, 1)
            dve.wait_ge(aggb_ps, 1)
            v.tensor_copy(aggb[:, :], ps[:, 2, 0:S]).then_inc(aggb_sb, 1)
            v.tensor_copy(ident16[:, :], ident)
            v.tensor_copy(causal16[:, :].rearrange("p (k m) -> p k m", m=S),
                          cst[:, C_CAUSAL:C_CAUSAL + S].unsqueeze(1).broadcast_to([P, D // S, S]))
            v.tensor_copy(vm[:, :, :, HD], seqmask.unsqueeze(1).broadcast_to([P, NKV, NB]))
            for n in range(S // NB):
                dve.wait_ge(mix_ps, n + 1)
                src = ps[:, n % 2, :].rearrange("p (o g b) -> p o g b", o=NB, b=NB)
                for i in range(NB):
                    last = v.tensor_tensor(mixw[:, :, :, n * NB + i], src[:, i, :, :],
                                           seqmask.unsqueeze(1).broadcast_to([P, G, NB]), ALU.mult)
                last.then_inc(mix_sb, 1)
            for c in range(KC):
                dve.wait_ge(wqkv_hi_sb, c + 1)
                minus(wqkv_lo[:, c, 0:D].rearrange("p (g k d) -> p g k d", g=NQ, k=NKV),
                      rawq[:, c, :].rearrange("p (k g d) -> p g k d", k=NKV, g=NQ),
                      wqkv_hi[:, c, 0:D].rearrange("p (g k d) -> p g k d", g=NQ, k=NKV))
            dve.wait_ge(wqkv_hi_sb, KC + 1)
            minus(wqkv_lo[:, :, D:D + 2 * P], rawkv, wqkv_hi[:, :, D:D + 2 * P])
            for j in range(PH):
                dve.wait_ge(base_hi_sb, j + 1)
                minus(base_lo[:, j, :], ps[:, 4 + j, :], base_hi[:, j, :]).then_inc(base_lo_sb, 1)
            dve.wait_ge(wo_hi_sb, NQ)
            for g in range(NQ):
                minus(wo_lo[:, g, :].rearrange("p (j n) -> p j n", j=PH),
                      rawo[:, g, :].rearrange("p (n j) -> p j n", j=PH),
                      wo_hi[:, g, :].rearrange("p (j n) -> p j n", j=PH))
            dve.wait_ge(cv_ps, 1)
            v.tensor_tensor(cvT[:, :, :], ps[:, 3, 0:TAPS * S].rearrange("p (k o) -> p k o", k=TAPS),
                            cst[:, C_CONV:C_CONV + S].unsqueeze(1).broadcast_to([P, TAPS, S]), ALU.mult).then_inc(cv_sb, 1)
            dve.wait_ge(cv_sb, 1)
            dve.wait_ge(convW_sb, 1)
            for j in range(PH):
                for s in range(SHIFTS):
                    for jo in range(PH):
                        tap = PH * (s - 1) + j - jo + PAD
                        if 0 <= tap < TAPS:
                            v.tensor_copy(convW[S * j:S * (j + 1), s, jo, :], cvT[S * j:S * (j + 1), tap, :])
            dve.wait_ge(ld["emap"], 16)
            v.tensor_copy(emapF[:, :], emapB[:, :]).then_inc(emapF_sb, 1)
            dve.wait_ge(emapF_sb, 1)
            v.tensor_tensor(selE[:, :, :], emapF[:, :].unsqueeze(1).broadcast_to([P, NE, NR]),
                            cst[:, C_E:C_E + NE].unsqueeze(2).broadcast_to([P, NE, NR]), ALU.is_equal).then_inc(emapF_sb, 1)
            dve.wait_ge(emapF_sb, 2)
            v.tensor_scalar(expert[:, :, :], selE[:, :, :], LORA_SCALE, None, ALU.mult).then_inc(emapF_sb, 1)
            for h in range(2):
                dve.wait_ge(ar_hi_sb, h + 1)
                minus(ar_lo[:, 2 * h:2 * h + 2, 0:P + NR],
                      ps[:, 4 + h, :].rearrange("p (c n) -> p c n", c=2)[:, :, 0:P + NR],
                      ar_hi[:, 2 * h:2 * h + 2, 0:P + NR])
            dve.wait_ge(lora_hi_sb, 1)
            minus(lora_lo[:, :], ps[:, 6, :], lora_hi[:, :]).then_inc(prep_sb, 1)
            dve.wait_ge(prep_sb, 1)
            dve.wait_ge(mixb_in, 16)
            dve.wait_ge(convb_in, 16)
            dve.wait_ge(ld["routerbB"], 16)

            def route(u):
                dve.wait_ge(ar_sb, u + 1)
                v.tensor_tensor(lg[:, :], arS[:, P:P + NR], routerbB[:, :], ALU.add).then_inc(lg_sb, 1)
                dve.wait_ge(lg_sb, u + 1)
                v.tensor_reduce(top[:, :], lg[:, :], AX.X, ALU.max).then_inc(top_sb, 1)
                dve.wait_ge(top_sb, u + 1)
                v.tensor_scalar(lgs[:, :], lg[:, :], top[:, :], None, ALU.subtract).then_inc(lgs_sb, 1)

            def route2(u):
                dve.wait_ge(ex_sb, u + 1)
                v.tensor_reduce(exZ[:, :], ex[:, :], AX.X, ALU.add)
                v.max(top2[:, :], ex[:, :]).then_inc(top2_sb, 1)
                dve.wait_ge(top2_sb, u + 1)
                v.reciprocal(exR[:, :], exZ[:, :])
                v.match_replace(out=rest[:, :], in_to_replace=top2[:, :], in_values=ex[:, :], imm_value=0.0).then_inc(rest_sb, 1)
                dve.wait_ge(rest_sb, u + 1)
                v.tensor_tensor(sel[:, :], ex[:, :], rest[:, :], ALU.subtract).then_inc(sel_sb, 1)
                dve.wait_ge(sel_sb, u + 1)
                v.tensor_tensor(selE[:, :, :], sel[:, :].unsqueeze(1).broadcast_to([P, NE, NR]), expert[:, :, :],
                                ALU.mult).then_inc(selE_sb, 1)
                dve.wait_ge(selE_sb, u + 1)
                v.tensor_reduce(we[:, :], selE[:, :, :], AX.X, ALU.add).then_inc(we_sb, 1)
                dve.wait_ge(we_sb, u + 1)
                v.scalar_tensor_tensor(hw[:, :, :], arS[:, 0:P].rearrange("p (e r) -> p e r", e=NE), exR[:, :],
                                       we[:, :].unsqueeze(2).broadcast_to([P, NE, RANK]), ALU.mult, ALU.mult
                                       ).then_inc(hw_sb, 1)

            def rope(t):
                dve.wait_ge(qkv_ps, t + 1)
                heads = (D + P) // HD
                src = ps[:, 0:2, :].rearrange("p a n -> p (a n)")[:, 0:D + P]
                a, b = (w.rearrange("p (h d) -> p h d", d=HD) for w in (t1, t2))
                src = src.rearrange("p (h d) -> p h d", d=HD)
                v.tensor_tensor(a, src, cst[:, C_COS:C_SIN].unsqueeze(1).broadcast_to([P, heads, HD]), ALU.mult)
                for to, of in ((0, HALF), (HALF, 0)):
                    last = v.tensor_tensor(b[:, :, to:to + HALF], src[:, :, of:of + HALF],
                                           cst[:, C_SIN + to:C_SIN + to + HALF].unsqueeze(1).broadcast_to([P, heads, HALF]),
                                           ALU.mult)
                last.then_inc(rope_t, 1)
                dve.wait_ge(rope_t, t + 1)
                v.tensor_tensor(qk[:, :], t1, t2, ALU.add).then_inc(qk_sb, 1)
                v.tensor_tensor(vm[:, :, :, 0:HD],
                                ps[:, 1, P:2 * P].rearrange("p (k d) -> p k d", d=HD).unsqueeze(2).broadcast_to([P, NKV, NB, HD]),
                                seqmask.unsqueeze(1).unsqueeze(3).broadcast_to([P, NKV, NB, HD]), ALU.mult).then_inc(vm_sb, 1)

            def keys(t):
                dve.wait_ge(qT_ps, t + 1)
                v.tensor_tensor(kT,
                                ps[:, 3, 0:P].rearrange("p (b m) -> p b m", m=S).unsqueeze(2).broadcast_to([P, NB, NKV, S]),
                                kvmask.unsqueeze(1).unsqueeze(3).broadcast_to([P, NB, NKV, S]), ALU.mult).then_inc(kT_sb, 1)

            def softmax(t):
                dve.wait_ge(s_ps, t + 1)
                s3 = ps[:, 0:2, :].rearrange("p a n -> p (a n)").rearrange("p (h m) -> p h m", m=S)
                v.tensor_reduce(mx[:, :], s3, AX.X, ALU.max).then_inc(mx_sb, 1)
                dve.wait_ge(mx_sb, t + 1)
                v.tensor_tensor(sx.rearrange("p (h m) -> p h m", m=S), s3,
                                mx[:, :].unsqueeze(2).broadcast_to([P, NB * NKV, S]), ALU.subtract).then_inc(sx_sb, 1)

            def normalize(t):
                dve.wait_ge(o_ps, t + 1)
                o5 = ps[:, 4:6, 0:4 * NB * VW].rearrange("p a (k b c) -> p a k b c", k=4, b=NB)
                for a in range(2):
                    last = v.reciprocal(rz[:, 4 * a:4 * a + 4, :], o5[:, a, :, :, HD])
                last.then_inc(rz_sb, 1)
                dve.wait_ge(rz_sb, t + 1)
                for a in range(2):
                    last = v.tensor_tensor(on.rearrange("p b (k d) -> p k b d", d=HD)[:, 4 * a:4 * a + 4, :, :],
                                           o5[:, a, :, :, 0:HD],
                                           rz[:, 4 * a:4 * a + 4, :].unsqueeze(3).broadcast_to([P, 4, NB, HD]), ALU.mult)
                last.then_inc(on_sb, 1)

            def steps(t):
                if live(t - 1):
                    dve.wait_ge(oT_ps, t)
                    dve.wait_ge(oT_hi_sb, t)
                    minus(oT_lo[:, :, :, :], ps[:, 6, :].rearrange("p (b g q) -> p g b q", b=NB, g=NQ),
                          oT_hi[:, :, :, :]).then_inc(oT_lo_sb, 1)
                if live(t - 2):
                    route(t - 2)
                    route2(t - 2)
                if live(t):
                    rope(t)
                if live(t - 1):
                    dve.wait_ge(wo_ps, t)
                    dve.wait_ge(xr_in, 16 * t)
                    wait(dve, x1b_sb, t - 1)
                    v.tensor_tensor(x1, ps[:, 4, :].rearrange("p (j n) -> p j n", j=PH),
                                    xr[:, :].rearrange("p (n j) -> p j n", j=PH), ALU.add).then_inc(x1_sb, 1)
                    dve.wait_ge(x1_sb, t)
                    by_phase(v.tensor_copy, (0, 2)).then_inc(ph_dve, 1)
                if live(t):
                    keys(t)
                if live(t - 2):
                    dve.wait_ge(hwT_hi_sb, t - 1)
                    minus(hwT_lo[:, :], ps[:, 7, 0:P], hwT_hi[:, :]).then_inc(hwT_lo_sb, 1)
                if live(t):
                    softmax(t)
                if live(t - 2):
                    dve.wait_ge(ffn_ps, t - 1)
                    dve.wait_ge(x1b_sb, t - 1)
                    wait(dve, out_st, 16 * (t - 2))
                    v.tensor_tensor(outS.rearrange("p (n j) -> p j n", j=PH),
                                    ps[:, 6, :].rearrange("p (j n) -> p j n", j=PH), x1b, ALU.add).then_inc(out_sb, 1)
                if live(t - 1):
                    dve.wait_ge(z_ps, t)
                    v.tensor_tensor(zs.rearrange("p (j n) -> p j n", j=PH), ps[:, 5, :].rearrange("p (j n) -> p j n", j=PH),
                                    convb[:, bass.ds((t - 1) * P, P)].unsqueeze(1).broadcast_to([P, PH, P]),
                                    ALU.add).then_inc(zs_sb, 1)
                if live(t + 1):
                    dve.wait_ge(y_ps, t + 2)
                    v.tensor_tensor(ys[:, :].rearrange("p (c n) -> p c n", c=KC), ps[:, 6, :].rearrange("p (c n) -> p c n", c=KC),
                                    mixb[:, bass.ds((t + 1) * P, P)].unsqueeze(1).broadcast_to([P, KC, P]),
                                    ALU.add).then_inc(ys_sb, 1)
                if live(t):
                    normalize(t)

            iterate(dve, steps)


_INS = ["x", "cond_128", "fside_S_0", "L0_cond_W0", "L0_cond_b0", "L0_cond_W1", "L0_cond_b1", "L0_cond_W2",
        "L0_cond_b2", "L0_cond_weight", "L0_cond_bias_k", "L0_attn_Wq", "L0_attn_Wk", "L0_attn_Wv", "L0_attn_Wo",
        "L0_cond2_weight", "L0_cond2_c_weight", "L0_ffn_base_W", "L0_ffn_base_b", "L0_ffn_router_W",
        "L0_ffn_router_b", "L0_ffn_A", "L0_ffn_B", "L0_ffn_expert_map"]


def kernel(**inputs):
    import concourse.bacc as bacc
    from concourse.bass_utils import run_bass_kernel_spmd

    nc = bacc.Bacc("TRN2", target_bir_lowering=False, num_devices=1)
    arrays, args = {}, []
    for name in _INS:
        arrays[name] = np.ascontiguousarray(inputs[name])
    arrays["const"] = constants()
    for name, a in arrays.items():
        args.append(nc.dram_tensor(name, a.shape, mybir.dt.from_np(a.dtype), kind="ExternalInput").ap())
    out = nc.dram_tensor("out", (B, S, D), F32, kind="ExternalOutput").ap()
    build(nc, *args, out)
    r = run_bass_kernel_spmd(nc, [arrays], core_ids=[0])
    return r.results[0]["out"]
```

```python
from contextlib import ExitStack

import numpy as np

import concourse.bass as bass
from concourse import mybir

F32 = mybir.dt.float32
F32R = mybir.dt.float32r
BF16 = mybir.dt.bfloat16
I32 = mybir.dt.int32
ALU = mybir.AluOpType
ACT = mybir.ActivationFunctionType
AX = mybir.AxisListType

P = 128
B = 128
S = 32
D = 512
NB = P // S
G = B // NB
HD = 16
HALF = HD // 2
NKV = 8
NQ = 4
KC = D // P
PH = 4
TAPS = 9
PAD = 4
SHIFTS = 3
CG = 8
NE = 8
RANK = 16
NR = 2 * NE - 1
NAR = 256
LORA_SCALE = 2.0
NCOND = 8
VW = HD + 1
MASKED = -1e30

C_ID = 0
C_CAUSAL = C_ID + P
C_KV = C_CAUSAL + S
C_SEQ = C_KV + NKV
C_CONV = C_SEQ + NB
C_COS = C_CONV + S
C_SIN = C_COS + HD
C_E = C_SIN + HD
C_N = C_E + NE


def constants():
    c = np.zeros((P, C_N), np.float32)
    r = np.arange(P)
    c[r, C_ID + r] = 1
    m = np.arange(S)
    c[:, C_CAUSAL:C_KV] = np.where(m[None, :] <= (r % S)[:, None], 0, MASKED)
    c[r, C_KV + r // HD] = 1
    c[r, C_SEQ + r // S] = 1
    c[:, C_CONV:C_COS] = (r % S // CG)[:, None] == (m // CG)[None, :]
    inv = (np.float32(1) / np.float32(10000.0) ** (np.arange(0, HD, 2, dtype=np.float32) / np.float32(HD))).astype(np.float32)
    angle = ((r % S).astype(np.float32)[:, None] * inv[None, :]).astype(np.float32)
    c[:, C_COS:C_SIN] = np.tile(np.cos(angle), 2)
    c[:, C_SIN:C_E] = np.concatenate([-np.sin(angle), np.sin(angle)], 1)
    c[:, C_E:C_N] = np.arange(NE)
    return c


def live(u):
    return not isinstance(u, int) or 0 <= u < G


def peeled(t, n):
    return isinstance(t, int) and t == n


def wait(eng, sem, count):
    if not isinstance(count, int) or count > 0:
        eng.wait_ge(sem, count)


def build(nc, x, cond, fside, cW0, cb0, cW1, cb1, cW2, cb2, cweight, cbias, Wq, Wk, Wv, Wo,
          convw, convc, baseW, baseb, routerW, routerb, loraA, loraB, emap, const, out):
    with ExitStack() as ctx:
        def sb(name, shape, dt=F32):
            return ctx.enter_context(nc.sbuf_tensor(name, shape, dt))

        def sem(name):
            return ctx.enter_context(nc.semaphore(name))

        cst = sb("cst", [P, C_N])
        ident = cst[:, C_ID:C_ID + P]
        kvmask = cst[:, C_KV:C_KV + NKV]
        seqmask = cst[:, C_SEQ:C_SEQ + NB]
        ident16 = sb("ident16", [P, P], BF16)
        causal16 = sb("causal16", [P, D], BF16)
        wqkv_hi = sb("wqkv_hi", [P, KC, D + 2 * P], F32R)
        wqkv_lo = sb("wqkv_lo", [P, KC, D + 2 * P], F32R)
        wo_hi = sb("wo_hi", [P, NQ, D], F32R)
        wo_lo = sb("wo_lo", [P, NQ, D], F32R)
        base_hi = sb("base_hi", [P, PH, D], F32R)
        base_lo = sb("base_lo", [P, PH, D], F32R)
        ar_hi = sb("ar_hi", [P, PH, NAR], F32R)
        ar_lo = sb("ar_lo", [P, PH, NAR], F32R)
        lora_hi = sb("lora_hi", [P, D], F32R)
        lora_lo = sb("lora_lo", [P, D], F32R)
        mixw = sb("mixw", [P, G, NB, S])
        mixb = sb("mixb", [P, B * S])
        convb = sb("convb", [P, B * S])
        convW = sb("convW", [P, SHIFTS, PH, S])
        basebB = sb("basebB", [P, D])
        routerbB = sb("routerbB", [P, NR])
        emapB = sb("emapB", [P, NR], I32)
        emapF = sb("emapF", [P, NR])
        expert = sb("expert", [P, NE, NR])

        raw = sb("raw", [P, 4096 + 3 * D])
        rawq = raw[:, 0:2048].rearrange("p (c n) -> p c n", c=KC)
        rawkv = raw[:, 2048:3072].rearrange("p (c n) -> p c n", c=KC)
        rawA = raw[:, 3072:3584]
        rawB = raw[:, 3584:4096].rearrange("p (j e r) -> p j e r", e=NE, j=PH)
        rawR = raw[:, 4096:4608]
        sx = raw[:, 0:1024]
        pr = raw[:, 1024:2048]
        prT = raw[:, 2048:3072].rearrange("p (k n) -> p k n", k=NKV)
        raw2 = sb("raw2", [P, 4 * D])
        rawo = raw2[:, :].rearrange("p (g n) -> p g n", g=NQ)
        on = raw2[:, 0:D].rearrange("p (b n) -> p b n", b=NB)
        x1 = raw2[:, D:2 * D].rearrange("p (j n) -> p j n", j=PH)
        x1b = raw2[:, 2 * D:3 * D].rearrange("p (j n) -> p j n", j=PH)
        outS = raw2[:, 3 * D:4 * D]
        raw3 = sb("raw3", [P, 4 * D])
        rawbase = raw3[:, :].rearrange("p (j n) -> p j n", j=PH)
        zs = raw3[:, 0:D]

        network = sb("network", [P, D + P])
        condS, cW0S, cW1S, h1, h2 = (network[:, P * n:P * n + P] for n in range(5))
        t1 = network[:, :]
        t2 = sb("t2", [P, D + P])
        condT = sb("condT", [P, P])
        ccS = sb("ccS", [S, P])
        ccT = sb("ccT", [P, S])
        cW2S = sb("cW2S", [P, NCOND])
        cb0S = sb("cb0S", [P, 1])
        cb1S = sb("cb1S", [P, 1])
        cb2B = sb("cb2B", [P, NCOND])
        cbiasS = sb("cbiasS", [NCOND, S])
        cwS = sb("cwS", [NCOND, S, S])
        fsideB = sb("fsideB", [P, S])
        att = sb("att", [P, NCOND])
        attE = sb("attE", [P, NCOND])
        attM = sb("attM", [P, 1])
        attZ = sb("attZ", [P, 1])
        attR = sb("attR", [P, 1])
        attT = sb("attT", [NCOND, P])
        aggb = sb("aggb", [P, S])
        ctxb = sb("ctxb", [P, S])
        cvS = sb("cvS", [S, CG * TAPS])
        cvT = sb("cvT", [P, TAPS, S])

        xm = sb("xm", [P, D])
        xr = sb("xr", [P, D])
        ys = sb("ys", [P, D])
        y_hi = sb("y_hi", [P, D], F32R)
        y_lo = sb("y_lo", [P, D], F32R)
        qk = sb("qk", [P, D + P])
        qk_t = sb("qk_t", [P, D + NB * NKV * S])
        qT = qk_t[:, 0:D].rearrange("p (b g q) -> p b g q", b=NB, g=NQ)
        kT = qk_t[:, D:].rearrange("p (b k m) -> p b k m", b=NB, k=NKV)
        cvR = qk_t[0:S, 0:TAPS * P].rearrange("o (k j g i) -> o k j g i", k=TAPS, j=NB, g=S // CG)
        cwR = convb[0:NCOND, :].rearrange("k (o b i) -> k o b i", o=S, b=NB)
        vm = sb("vm", [P, NKV, NB, VW])
        mx = sb("mx", [P, NB * NKV])
        rz = sb("rz", [P, NKV, NB])
        oT_hi = sb("oT_hi", [P, NQ, NB, S], F32R)
        oT_lo = sb("oT_lo", [P, NQ, NB, S], F32R)
        x1ph = sb("x1ph", [P, NB, P + 2])
        z_hi = sb("z_hi", [P, PH, P], F32R)
        z_lo = sb("z_lo", [P, PH, P], F32R)
        arS = sb("arS", [P, NAR])
        lg = sb("lg", [P, NR])
        lgs = sb("lgs", [P, NR])
        ex = sb("ex", [P, NR])
        exZ = sb("exZ", [P, 1])
        exR = sb("exR", [P, 1])
        top = sb("top", [P, 1])
        top2 = sb("top2", [P, 8])
        rest = sb("rest", [P, NR])
        sel = sb("sel", [P, NR])
        selE = sb("selE", [P, NE, NR])
        we = sb("we", [P, NE])
        hw = sb("hw", [P, NE, RANK])
        hwT_hi = sb("hwT_hi", [P, P], F32R)
        hwT_lo = sb("hwT_lo", [P, P], F32R)

        mixb_dram = nc.dram_tensor("mixb_dram", [B, S], F32, kind="Internal").ap()
        convb_dram = nc.dram_tensor("convb_dram", [B, S], F32, kind="Internal").ap()

        bank = [ctx.enter_context(nc.psum_tensor(f"bank{i}", [P, 512], F32)) for i in range(0)]
        ps = ctx.enter_context(nc.psum_tensor("ps", [P, 8, 512], F32))

        names = ("const cond cc fside cW0 cW1 cW2 cb0 cb1 cb2 cbias cw wq wkv wo base A B R convw basebB "
                 "routerbB emap").split()
        ld = {n: sem("ld_" + n) for n in names}
        cT_ps, cT_sb, cc_ps, cc_sb = sem("cT_ps"), sem("cT_sb"), sem("cc_ps"), sem("cc_sb")
        mixb_in2, wq_lo_pool, pads_sb, q_ps = sem("mixb_in2"), sem("wq_lo_pool"), sem("pads_sb"), sem("q_ps")
        h1_ps, h1_sb, h2_ps, h2_sb = sem("h1_ps"), sem("h1_sb"), sem("h2_ps"), sem("h2_sb")
        lg_ps, aM, aE, aZ, att_sb = sem("lg_ps"), sem("aM"), sem("aE"), sem("aZ"), sem("att_sb")
        attT_ps, attT_sb = sem("attT_ps"), sem("attT_sb")
        ctx_ps, ctx_sb, aggb_ps, aggb_sb = sem("ctx_ps"), sem("ctx_sb"), sem("aggb_ps"), sem("aggb_sb")
        ctx_dram, aggb_dram, mixb_in, convb_in = sem("ctx_dram"), sem("aggb_dram"), sem("mixb_in"), sem("convb_in")
        cwR_sb, cvR_sb, cv_ps, cv_sb = sem("cwR_sb"), sem("cvR_sb"), sem("cv_ps"), sem("cv_sb")
        baseT_ps, arT_ps, loraT_ps = sem("baseT_ps"), sem("arT_ps"), sem("loraT_ps")
        base_hi_sb, base_lo_sb = sem("base_hi_sb"), sem("base_lo_sb")
        ar_hi_sb, ar_lo_sb, lora_hi_sb, lora_lo_sb = sem("ar_hi_sb"), sem("ar_lo_sb"), sem("lora_hi_sb"), sem("lora_lo_sb")
        wqkv_hi_sb, wqkv_lo_sb, wo_hi_sb, wo_lo_sb = sem("wqkv_hi_sb"), sem("wqkv_lo_sb"), sem("wo_hi_sb"), sem("wo_lo_sb")
        mix_ps, mix_sb, masks_sb, emapF_sb, prep_sb = sem("mix_ps"), sem("mix_sb"), sem("masks_sb"), sem("emapF_sb"), sem("prep_sb")

        xm_in, xr_in, out_st = sem("xm_in"), sem("xr_in"), sem("out_st")
        ph_act, ph_dve = sem("ph_act"), sem("ph_dve")
        y_ps, ys_sb, y_hi_sb, y_lo_sb = sem("y_ps"), sem("ys_sb"), sem("y_hi_sb"), sem("y_lo_sb")
        qkv_ps, rope_t, qk_sb, vm_sb = sem("qkv_ps"), sem("rope_t"), sem("qk_sb"), sem("vm_sb")
        qT_ps, qT_sb, kT_sb = sem("qT_ps"), sem("qT_sb"), sem("kT_sb")
        s_ps, mx_sb, sx_sb, p_sb = sem("s_ps"), sem("mx_sb"), sem("sx_sb"), sem("p_sb")
        pT_ps, pT_sb, o_ps, rz_sb, on_sb = sem("pT_ps"), sem("pT_sb"), sem("o_ps"), sem("rz_sb"), sem("on_sb")
        oT_ps, oT_hi_sb, oT_lo_sb = sem("oT_ps"), sem("oT_hi_sb"), sem("oT_lo_sb")
        wo_ps, x1_sb, x1b_sb = sem("wo_ps"), sem("x1_sb"), sem("x1b_sb")
        z_ps, zs_sb, z_hi_sb, z_lo_sb = sem("z_ps"), sem("zs_sb"), sem("z_hi_sb"), sem("z_lo_sb")
        ar_ps, ar_sb, lg_sb, top_sb, lgs_sb = sem("ar_ps"), sem("ar_sb"), sem("lg_sb"), sem("top_sb"), sem("lgs_sb")
        ex_sb, top2_sb, rest_sb, sel_sb, selE_sb = sem("ex_sb"), sem("top2_sb"), sem("rest_sb"), sem("sel_sb"), sem("selE_sb")
        we_sb, hw_sb, hwT_ps, hwT_hi_sb, hwT_lo_sb = sem("we_sb"), sem("hw_sb"), sem("hwT_ps"), sem("hwT_hi_sb"), sem("hwT_lo_sb")
        ffn_ps, out_sb = sem("ffn_ps"), sem("out_sb")

        x_g = x.rearrange("(g b) s d -> g (b s) d", b=NB)
        out_g = out.rearrange("(g b) s d -> g (b s) d", b=NB)

        def group(ap, u):
            return ap[bass.ds(u, 1), :, :].rearrange("a p n -> (a p) n")

        def iterate(eng, steps):
            for t in range(-1, 3):
                steps(t)
            with eng.Fori(3, G - 1) as t:
                steps(t)
            for t in range(G - 1, G + 2):
                steps(t)

        def by_phase(copy, phases):
            for j in phases:
                for b in range(NB):
                    last = copy(x1ph[S * j:S * (j + 1), b, 1:P + 1], x1[S * b:S * (b + 1), j, :])
            return last

        block = ctx.enter_context(nc.Block())

        @block.sync
        def _(sp):
            sp.dma_start(condS[:, :], cond).then_inc(ld["cond"], 16)
            sp.dma_start(cst[:, :], const).then_inc(ld["const"], 16)
            sp.dma_start(cW0S[:, :], cW0).then_inc(ld["cW0"], 16)
            sp.dma_start(cb0S[:, :], cb0.rearrange("(p a) -> p a", a=1)).then_inc(ld["cb0"], 16)
            sp.dma_start(cW1S[:, :], cW1).then_inc(ld["cW1"], 16)
            sp.dma_start(cb1S[:, :], cb1.rearrange("(p a) -> p a", a=1)).then_inc(ld["cb1"], 16)
            sp.dma_start(cW2S[:, :], cW2).then_inc(ld["cW2"], 16)
            sp.dma_start(cb2B[:, :], cb2.partition_broadcast(P)).then_inc(ld["cb2"], 16)
            sp.dma_start(cwS[:, :, :], cweight.rearrange("k o i a -> k o (i a)")).then_inc(ld["cw"], 16)
            sp.dma_start(cbiasS[:, :], cbias).then_inc(ld["cbias"], 16)
            sp.dma_start(xm[:, :], group(x_g, 0)).then_inc(xm_in, 16)
            sp.dma_start(ccS[:, :], convc).then_inc(ld["cc"], 16)
            sp.dma_start(fsideB[:, :], fside.partition_broadcast(P)).then_inc(ld["fside"], 16)
            sp.dma_start(cvS[:, :], convw.rearrange("o i k -> o (i k)")).then_inc(ld["convw"], 16)
            sp.dma_start(rawbase, baseW.rearrange("(p j) l -> p j l", j=PH)).then_inc(ld["base"], 16)
            sp.wait_ge(aggb_sb, 1)
            sp.dma_start(mixb_dram, aggb[:, :]).then_inc(aggb_dram, 16)
            sp.wait_ge(ctx_sb, 1)
            sp.dma_start(convb_dram, ctxb[:, :]).then_inc(ctx_dram, 16)
            sp.wait_ge(aggb_dram, 16)
            mixb_row = mixb_dram.rearrange("b s -> (b s)")
            sp.dma_start(mixb[:, 0:P], mixb_row[0:P].partition_broadcast(P)).then_inc(mixb_in, 16)
            sp.dma_start(mixb[:, P:], mixb_row[P:].partition_broadcast(P)).then_inc(mixb_in2, 16)
            sp.wait_ge(mix_ps, S // NB)
            sp.wait_ge(ctx_dram, 16)
            sp.dma_start(convb[:, :], convb_dram.rearrange("b s -> (b s)").partition_broadcast(P)).then_inc(convb_in, 16)

            def steps(t):
                if live(t - 1):
                    wait(sp, x1_sb, t - 1)
                    sp.dma_start(xr[:, :], group(x_g, t - 1)).then_inc(xr_in, 16)
                if live(t - 2):
                    wait(sp, out_sb, t - 1)
                    sp.dma_start(group(out_g, t - 2), outS).then_inc(out_st, 16)
                if live(t + 1) and live(t + 2):
                    wait(sp, y_ps, t + 2)
                    sp.dma_start(xm[:, :], group(x_g, t + 2)).then_inc(xm_in, 16)

            for t in range(-1, 3):
                steps(t)
            with sp.Fori(3, G - 2) as t:
                steps(t)
            for t in range(G - 2, G + 2):
                steps(t)
            sp.wait_ge(out_st, 16 * G)

        @block.tensor
        def _(pe):
            mm = nc.tensor.matmul

            def product(dst, left, right):
                n = 0
                for c in range(len(left)):
                    (lh, ll), (rh, rl) = left[c], right[c]
                    for a, b in ((lh, rh), (lh, rl), (ll, rh)):
                        last = mm(dst, a, b, start=(n == 0), stop=(n == 3 * len(left) - 1))
                        n += 1
                return last

            pe.wait_ge(ld["const"], 16)
            pe.wait_ge(ld["cond"], 16)
            nc.tensor.transpose(ps[:, 0, 0:P], condS[:, :], ident).then_inc(cT_ps, 1)
            pe.wait_ge(cT_sb, 1)
            pe.wait_ge(ld["cW0"], 16)
            mm(ps[:, 1, 0:P], cW0S[:, :], condT[:, :], start=True, stop=True).then_inc(h1_ps, 1)
            pe.wait_ge(ld["cW1"], 16)
            pe.wait_ge(h1_sb, 1)
            mm(ps[:, 1, 0:P], cW1S[:, :], h1[:, :], start=True, stop=True).then_inc(h2_ps, 1)
            pe.wait_ge(ld["cW2"], 16)
            pe.wait_ge(h2_sb, 1)
            mm(ps[:, 1, 0:NCOND], h2[:, :], cW2S[:, :], start=True, stop=True).then_inc(lg_ps, 1)
            pe.wait_ge(ld["cc"], 16)
            nc.tensor.transpose(ps[:, 3, 0:S], ccS[:, :], cst[0:S, C_ID:C_ID + S]).then_inc(cc_ps, 1)
            pe.wait_ge(att_sb, 1)
            nc.tensor.transpose(ps[0:NCOND, 0, 0:P], att[:, :], ident).then_inc(attT_ps, 1)
            pe.wait_ge(cc_sb, 1)
            mm(ps[:, 7, 0:S], condT[:, :], ccT[:, :], start=True, stop=True).then_inc(ctx_ps, 1)
            pe.wait_ge(attT_sb, 1)
            pe.wait_ge(ld["cbias"], 16)
            mm(ps[:, 2, 0:S], attT[:, :], cbiasS[:, :], start=True, stop=True).then_inc(aggb_ps, 1)
            pe.wait_ge(cwR_sb, 1)
            for n in range(S // NB):
                if n >= 4:
                    pe.wait_ge(mix_sb, n - 3)
                for i in range(NB):
                    last = mm(ps[:, 3 + n % 4, i * P:(i + 1) * P],
                              cwR[:, n * NB + i, :, :].rearrange("k b i -> k (b i)"), attT[:, :],
                              start=True, stop=True)
                last.then_inc(mix_ps, 1)
            pe.wait_ge(mix_sb, S // NB)

            def prepare_conv():
                pe.wait_ge(cvR_sb, 1)
                pe.wait_ge(ctx_sb, 1)
                for k in range(TAPS):
                    last = nc.tensor.transpose(ps[:, 7, (TAPS - 1 - k) * S:(TAPS - k) * S],
                                               cvR[:, k, :, :, :].rearrange("o j g i -> o (j g i)"),
                                               cst[0:S, C_ID:C_ID + S])
                last.then_inc(cv_ps, 1)

            def prepare_base(phases):
                pe.wait_ge(ld["base"], 16)
                for j in phases:
                    if j >= 2:
                        pe.wait_ge(base_lo_sb, j - 1)
                    for jo in range(PH):
                        last = nc.tensor.transpose(ps[:, 4 + j % 2, jo * P:(jo + 1) * P],
                                                   rawbase[:, jo, :].rearrange("o (p j) -> o j p", j=PH)[:, j, :],
                                                   ident)
                    last.then_inc(baseT_ps, 1)

            def prepare_ar():
                pe.wait_ge(ld["A"], 16)
                pe.wait_ge(ld["R"], 16)
                for j in range(PH):
                    if j % 2 == 0:
                        pe.wait_ge(base_lo_sb, 3 + j // 2)
                    at = ps[:, 4 + j // 2, :].rearrange("p (c n) -> p c n", c=2)[:, j % 2, :]
                    nc.tensor.transpose(at[:, 0:P], rawA.rearrange("o (p j) -> o j p", j=PH)[:, j, :], ident)
                    last = nc.tensor.transpose(at[:, P:P + NR],
                                               rawR[0:NR, :].rearrange("o (p j) -> o j p", j=PH)[:, j, :],
                                               cst[0:NR, C_ID:C_ID + NR])
                    if j % 2:
                        last.then_inc(arT_ps, 1)

            def prepare_lora():
                pe.wait_ge(ld["B"], 16 * PH)
                pe.wait_ge(cv_sb, 1)
                for j in range(PH):
                    last = nc.tensor.transpose(ps[:, 7, j * P:(j + 1) * P],
                                               rawB[:, j, :, :].rearrange("p e r -> p (e r)"), ident)
                last.then_inc(loraT_ps, 1)

            def mix(u):
                pe.wait_ge(xm_in, 16 * (u + 1))
                wait(pe, out_sb, u - 2)
                for c in range(KC):
                    last = mm(ps[:, 6, c * P:(c + 1) * P], xm[:, c * P:(c + 1) * P],
                              mixw[:, bass.ds(u, 1), :, :].rearrange("p a b o -> p (a b o)"),
                              start=True, stop=True)
                last.then_inc(y_ps, 1)

            def qkv(t):
                pe.wait_ge(y_hi_sb, t + 1)
                pe.wait_ge(y_lo_sb, t + 1)
                wait(pe, sx_sb, 2 * t)
                y = [(y_hi[:, c * P:(c + 1) * P], y_lo[:, c * P:(c + 1) * P]) for c in range(KC)]
                if peeled(t, 0):
                    pe.wait_ge(wqkv_hi_sb, KC + 1)
                    pe.wait_ge(wqkv_lo_sb, KC // 2 + 1)
                    pe.wait_ge(wq_lo_pool, KC // 2)
                product(ps[:, 0, :], y, [(wqkv_hi[:, c, 0:D], wqkv_lo[:, c, 0:D]) for c in range(KC)]
                        ).then_inc(q_ps, 1)
                product(ps[:, 1, 0:2 * P], y,
                        [(wqkv_hi[:, c, D:D + 2 * P], wqkv_lo[:, c, D:D + 2 * P]) for c in range(KC)]
                        ).then_inc(qkv_ps, 1)

            def project(u):
                pe.wait_ge(oT_hi_sb, u + 1)
                pe.wait_ge(oT_lo_sb, u + 1)
                o = [tuple(w[:, g, :, :].rearrange("p b q -> p (b q)") for w in (oT_hi, oT_lo)) for g in range(NQ)]
                product(ps[:, 4, :], o, [(wo_hi[:, g, :], wo_lo[:, g, :]) for g in range(NQ)]).then_inc(wo_ps, 1)

            def transpose_qk(t):
                pe.wait_ge(qk_sb, t + 1)
                for g in range(NQ):
                    nc.tensor.transpose(ps[:, 2, g * P:(g + 1) * P], qk[:, g * P:(g + 1) * P], ident)
                nc.tensor.transpose(ps[:, 3, 0:P], qk[:, D:D + P], ident).then_inc(qT_ps, 1)

            def transpose_hw(u):
                pe.wait_ge(hw_sb, u + 1)
                nc.tensor.transpose(ps[:, 7, 0:P], hw[:, :, :].rearrange("p e r -> p (e r)"), ident).then_inc(hwT_ps, 1)

            def base(u):
                z = [(z_hi[:, j, :], z_lo[:, j, :]) for j in range(PH)]
                n = 0
                for j in range(PH):
                    for a, b in ((z_hi, base_hi), (z_hi, base_lo), (z_lo, base_hi)):
                        mm(ps[:, 6, :], a[:, j, :], b[:, j, :], start=(n == 0), stop=False)
                        n += 1

            def scores(t):
                pe.wait_ge(qT_sb, t + 1)
                pe.wait_ge(kT_sb, t + 1)
                pe.wait_ge(vm_sb, t + 1)
                for h in range(2):
                    mm(ps[:, h, :], ident16[:, :], causal16[:, :], start=True, stop=False)
                    for b in (2 * h, 2 * h + 1):
                        last = mm(ps[:, h, (b % 2) * 256:(b % 2) * 256 + 256], qT[:, b, :, :].rearrange("p g q -> p (g q)"),
                                  kT[:, b, :, :].rearrange("p k m -> p (k m)"), start=False, stop=(b % 2 == 1))
                    last.then_inc(s_ps, 1)

            def lora(u):
                pe.wait_ge(hwT_hi_sb, u + 1)
                pe.wait_ge(hwT_lo_sb, u + 1)
                mm(ps[:, 6, :], hwT_hi[:, :], lora_hi[:, :], start=False, stop=False)
                mm(ps[:, 6, :], hwT_hi[:, :], lora_lo[:, :], start=False, stop=False)
                mm(ps[:, 6, :], hwT_lo[:, :], lora_hi[:, :], start=False, stop=True).then_inc(ffn_ps, 1)

            def conv(u):
                pe.wait_ge(ph_act, u + 1)
                pe.wait_ge(ph_dve, u + 1)
                zo = ps[:, 5, :].rearrange("p (j t) -> p j t", j=PH)
                for b in range(NB):
                    for s in range(SHIFTS):
                        last = mm(zo[:, :, b * S:(b + 1) * S], x1ph[:, b, s:s + P],
                                  convW[:, s, :, :], start=(s == 0), stop=(s == SHIFTS - 1))
                last.then_inc(z_ps, 1)

            def transpose_p(t):
                pe.wait_ge(p_sb, 2 * (t + 1))
                for k in range(NKV):
                    last = nc.tensor.transpose(ps[:, 2 + k // 4, (k % 4) * P:(k % 4 + 1) * P], pr[:, k * P:(k + 1) * P], ident)
                    if k % 4 == 3:
                        last.then_inc(pT_ps, 1)

            def values(t):
                wait(pe, zs_sb, t)
                for k in range(NKV):
                    if k % 4 == 0:
                        pe.wait_ge(pT_sb, 2 * t + 1 + k // 4)
                    last = mm(ps[:, 4 + k // 4, (k % 4) * NB * VW:(k % 4 + 1) * NB * VW], prT[:, k, :],
                              vm[:, k, :, :].rearrange("p b c -> p (b c)"), start=True, stop=True)
                    if k % 4 == 3:
                        last.then_inc(o_ps, 1)

            def heads(u):
                pe.wait_ge(z_hi_sb, u + 1)
                pe.wait_ge(z_lo_sb, u + 1)
                z = [(z_hi[:, j, :], z_lo[:, j, :]) for j in range(PH)]
                product(ps[:, 7, 0:NAR], z, [(ar_hi[:, j, :], ar_lo[:, j, :]) for j in range(PH)]).then_inc(ar_ps, 1)

            def transpose_o(t):
                pe.wait_ge(on_sb, t + 1)
                wait(pe, ys_sb, t + 2 if live(t + 1) else 0)
                for b in range(NB):
                    last = nc.tensor.transpose(ps[:, 6, b * P:(b + 1) * P], on[:, b, :], ident)
                last.then_inc(oT_ps, 1)

            def steps(t):
                if live(t):
                    qkv(t)
                if peeled(t, 0):
                    prepare_conv()
                    prepare_base((0, 1))
                if peeled(t, 1):
                    pe.wait_ge(wo_hi_sb, NQ)
                    pe.wait_ge(wo_lo_sb, NQ)
                if live(t - 1):
                    project(t - 1)
                if live(t):
                    transpose_qk(t)
                if peeled(t, 0):
                    prepare_base((2, 3))
                    prepare_lora()
                if live(t - 2):
                    base(t - 2)
                    transpose_hw(t - 2)
                if live(t):
                    scores(t)
                if peeled(t, 0):
                    prepare_ar()
                if live(t - 2):
                    lora(t - 2)
                if live(t - 1):
                    conv(t - 1)
                if live(t):
                    transpose_p(t)
                if live(t + 1):
                    mix(t + 1)
                if peeled(t, 0):
                    pe.wait_ge(prep_sb, 1)
                if live(t):
                    values(t)
                if live(t - 1):
                    heads(t - 1)
                if live(t):
                    transpose_o(t)

            iterate(pe, steps)

        @block.scalar
        def _(act):
            act.dma_start(rawq, Wq.rearrange("(c p) n -> p c n", p=P)).then_inc(ld["wq"], 16)
            act.dma_start(rawkv[:, :, 0:P], Wk.rearrange("(c p) n -> p c n", p=P)).then_inc(ld["wkv"], 16)
            act.dma_start(rawkv[:, :, P:2 * P], Wv.rearrange("(c p) n -> p c n", p=P)).then_inc(ld["wkv"], 16)

            def copy(dst, src):
                return nc.scalar.activation(dst, src, ACT.Copy)

            act.wait_ge(h1_ps, 1)
            act.wait_ge(ld["cb0"], 16)
            nc.scalar.activation(h1[:, :], ps[:, 1, 0:P], ACT.Gelu, bias=cb0S[:, :]).then_inc(h1_sb, 1)
            act.wait_ge(h2_ps, 1)
            act.wait_ge(ld["cb1"], 16)
            nc.scalar.activation(h2[:, :], ps[:, 1, 0:P], ACT.Gelu, bias=cb1S[:, :]).then_inc(h2_sb, 1)
            act.wait_ge(aM, 1)
            nc.scalar.activation(attE[:, :], att[:, :], ACT.Exp, bias=attM[:, :], accum_out=attZ[:, :]).then_inc(aE, 1)
            act.wait_ge(ld["wq"], 16)
            for c in range(KC):
                copy(wqkv_hi[:, c, 0:D].rearrange("p (g k d) -> p g k d", g=NQ, k=NKV),
                     rawq[:, c, :].rearrange("p (k g d) -> p g k d", k=NKV, g=NQ)).then_inc(wqkv_hi_sb, 1)
            act.wait_ge(ld["wkv"], 32)
            copy(wqkv_hi[:, :, D:D + 2 * P], rawkv).then_inc(wqkv_hi_sb, 1)

            def prepare_wo():
                act.wait_ge(ld["wo"], 16 * NKV)
                for g in range(NQ):
                    copy(wo_hi[:, g, :].rearrange("p (j n) -> p j n", j=PH),
                         rawo[:, g, :].rearrange("p (n j) -> p j n", j=PH)).then_inc(wo_hi_sb, 1)

            def prepare_base(phases):
                for j in phases:
                    act.wait_ge(baseT_ps, j + 1)
                    copy(base_hi[:, j, :], ps[:, 4 + j % 2, :]).then_inc(base_hi_sb, 1)

            def prepare_lora():
                act.wait_ge(loraT_ps, 1)
                copy(lora_hi[:, :], ps[:, 7, :]).then_inc(lora_hi_sb, 1)

            def prepare_ar():
                for h in range(2):
                    act.wait_ge(arT_ps, h + 1)
                    act.wait_ge(pads_sb, 1)
                    copy(ar_hi[:, 2 * h:2 * h + 2, 0:P + NR],
                         ps[:, 4 + h, :].rearrange("p (c n) -> p c n", c=2)[:, :, 0:P + NR]).then_inc(ar_hi_sb, 1)

            def steps(t):
                if live(t - 1):
                    act.wait_ge(oT_ps, t)
                    copy(oT_hi[:, :, :, :], ps[:, 6, :].rearrange("p (b g q) -> p g b q", b=NB, g=NQ)).then_inc(oT_hi_sb, 1)
                if live(t - 2):
                    act.wait_ge(lgs_sb, t - 1)
                    nc.scalar.activation(ex[:, :], lgs[:, :], ACT.Exp).then_inc(ex_sb, 1)
                if peeled(t, 0):
                    prepare_wo()
                    prepare_base((0, 1))
                if live(t):
                    act.wait_ge(qT_ps, t + 1)
                    copy(qT, ps[:, 2, :].rearrange("p (g b q) -> p b g q", g=NQ, b=NB)).then_inc(qT_sb, 1)
                if live(t - 1):
                    act.wait_ge(x1_sb, t)
                    by_phase(copy, (1, 3)).then_inc(ph_act, 1)
                if live(t - 2):
                    act.wait_ge(hwT_ps, t - 1)
                    copy(hwT_hi[:, :], ps[:, 7, 0:P]).then_inc(hwT_hi_sb, 1)
                if peeled(t, 0):
                    prepare_base((2, 3))
                    prepare_lora()
                if live(t):
                    for h in range(2):
                        act.wait_ge(sx_sb, 2 * t + 1 + h)
                        nc.scalar.activation(pr.rearrange("p (k b m) -> p b k m", k=NKV, b=NB)[:, 2 * h:2 * h + 2, :, :],
                                             sx.rearrange("p (b k m) -> p b k m", b=NB, k=NKV)[:, 2 * h:2 * h + 2, :, :],
                                             ACT.Exp, scale=HD ** -0.5).then_inc(p_sb, 1)
                if peeled(t, 0):
                    prepare_ar()
                if live(t):
                    for h in range(2):
                        act.wait_ge(pT_ps, 2 * t + 1 + h)
                        copy(prT[:, 4 * h:4 * h + 4, :].rearrange("p k n -> p (k n)"), ps[:, 2 + h, :]).then_inc(pT_sb, 1)
                if live(t - 1):
                    act.wait_ge(zs_sb, t)
                    copy(z_hi[:, :, :].rearrange("p j n -> p (j n)"), zs).then_inc(z_hi_sb, 1)
                if live(t + 1):
                    act.wait_ge(ys_sb, t + 2)
                    copy(y_hi[:, :], ys[:, :]).then_inc(y_hi_sb, 1)
                if live(t - 1):
                    act.wait_ge(ar_ps, t)
                    copy(arS[:, :], ps[:, 7, 0:NAR]).then_inc(ar_sb, 1)

            iterate(act, steps)

        @block.gpsimd
        def _(pool):
            for k in range(NKV):
                pool.dma_start(rawo[HD * k:HD * (k + 1), :, :],
                               Wo.rearrange("(k g d) n -> k d g n", k=NKV, g=NQ)[k]).then_inc(ld["wo"], 16)
            nc.gpsimd.memset(x1ph[:, :, :], 0.0)
            nc.gpsimd.memset(ar_hi[:, :, P + NR:NAR].bitcast(F32), 0.0)
            nc.gpsimd.memset(ar_lo[:, :, P + NR:NAR].bitcast(F32), 0.0)
            nc.gpsimd.memset(convW[:, :, :, :], 0.0).then_inc(pads_sb, 1)
            pool.dma_start(rawA, loraA.rearrange("e r l -> (e r) l")).then_inc(ld["A"], 16)
            pool.dma_start(rawR[0:NR, :], routerW).then_inc(ld["R"], 16)
            for j in range(PH):
                pool.dma_start(rawB[:, j, :, :], loraB.rearrange("e (p j) r -> j p e r", j=PH)[j]).then_inc(ld["B"], 16)
            pool.dma_start(emapB[:, :], emap.partition_broadcast(P)).then_inc(ld["emap"], 16)
            pool.dma_start(routerbB[:, :], routerb.partition_broadcast(P)).then_inc(ld["routerbB"], 16)
            pool.dma_start(basebB[:, :], baseb.partition_broadcast(P)).then_inc(ld["basebB"], 16)
            for c in range(KC // 2, KC):
                pool.wait_ge(wqkv_hi_sb, c + 1)
                nc.gpsimd.tensor_tensor(wqkv_lo[:, c, 0:D].rearrange("p (g k d) -> p g k d", g=NQ, k=NKV),
                                        rawq[:, c, :].rearrange("p (k g d) -> p g k d", k=NKV, g=NQ),
                                        wqkv_hi[:, c, 0:D].rearrange("p (g k d) -> p g k d", g=NQ, k=NKV).bitcast(F32),
                                        ALU.subtract).then_inc(wq_lo_pool, 1)

            def prepare_wo():
                for g in range(NQ):
                    pool.wait_ge(wo_hi_sb, g + 1)
                    nc.gpsimd.tensor_tensor(wo_lo[:, g, :].rearrange("p (j n) -> p j n", j=PH),
                                            rawo[:, g, :].rearrange("p (n j) -> p j n", j=PH),
                                            wo_hi[:, g, :].rearrange("p (j n) -> p j n", j=PH).bitcast(F32),
                                            ALU.subtract).then_inc(wo_lo_sb, 1)

            def steps(t):
                if peeled(t, 0):
                    prepare_wo()
                if live(t - 1):
                    pool.wait_ge(zs_sb, t)
                    pool.wait_ge(z_hi_sb, t)
                    nc.gpsimd.tensor_tensor(z_lo[:, :, :].rearrange("p j n -> p (j n)"), zs,
                                            z_hi[:, :, :].rearrange("p j n -> p (j n)").bitcast(F32),
                                            ALU.subtract).then_inc(z_lo_sb, 1)
                if live(t + 1):
                    pool.wait_ge(y_hi_sb, t + 2)
                    nc.gpsimd.tensor_tensor(y_lo[:, :], ys[:, :], y_hi[:, :].bitcast(F32),
                                            ALU.subtract).then_inc(y_lo_sb, 1)
                if live(t - 1):
                    pool.wait_ge(x1_sb, t)
                    pool.wait_ge(ld["basebB"], 16)
                    wait(pool, out_sb, t - 1)
                    nc.gpsimd.tensor_tensor(x1b, x1, basebB[:, :].rearrange("p (n j) -> p j n", j=PH),
                                            ALU.add).then_inc(x1b_sb, 1)

            iterate(pool, steps)

        @block.vector
        def _(dve):
            v = nc.vector

            def minus(dst, value, hi):
                return v.tensor_tensor(dst, value, hi.bitcast(F32), ALU.subtract)

            dve.wait_ge(cT_ps, 1)
            v.tensor_copy(condT[:, :], ps[:, 0, 0:P]).then_inc(cT_sb, 1)
            v.tensor_copy(ident16[:, :], ident)
            v.tensor_copy(causal16[:, :].rearrange("p (k m) -> p k m", m=S),
                          cst[:, C_CAUSAL:C_CAUSAL + S].unsqueeze(1).broadcast_to([P, D // S, S]))
            v.tensor_copy(vm[:, :, :, HD], seqmask.unsqueeze(1).broadcast_to([P, NKV, NB]))
            dve.wait_ge(ld["cw"], 16)
            v.tensor_copy(cwR, cwS[:, :, :].unsqueeze(2).broadcast_to([NCOND, S, NB, S])).then_inc(cwR_sb, 1)
            dve.wait_ge(lg_ps, 1)
            dve.wait_ge(ld["cb2"], 16)
            v.tensor_tensor(att[:, :], ps[:, 1, 0:NCOND], cb2B[:, :], ALU.add).then_inc(aZ, 1)
            dve.wait_ge(aZ, 1)
            v.tensor_reduce(attM[:, :], att[:, :], AX.X, ALU.max, negate=True).then_inc(aM, 1)
            dve.wait_ge(aE, 1)
            v.reciprocal(attR[:, :], attZ[:, :]).then_inc(aZ, 1)
            dve.wait_ge(aZ, 2)
            v.tensor_scalar(att[:, :], attE[:, :], attR[:, :], None, ALU.mult).then_inc(att_sb, 1)
            dve.wait_ge(cc_ps, 1)
            v.tensor_copy(ccT[:, :], ps[:, 3, 0:S]).then_inc(cc_sb, 1)
            dve.wait_ge(attT_ps, 1)
            v.tensor_copy(attT[:, :], ps[0:NCOND, 0, 0:P]).then_inc(attT_sb, 1)
            dve.wait_ge(aggb_ps, 1)
            v.tensor_copy(aggb[:, :], ps[:, 2, 0:S]).then_inc(aggb_sb, 1)
            dve.wait_ge(ctx_ps, 1)
            dve.wait_ge(ld["fside"], 16)
            v.tensor_tensor(ctxb[:, :], ps[:, 7, 0:S], fsideB[:, :], ALU.add).then_inc(ctx_sb, 1)
            for n in range(S // NB):
                dve.wait_ge(mix_ps, n + 1)
                src = ps[:, 3 + n % 4, :].rearrange("p (o g b) -> p o g b", o=NB, b=NB)
                for i in range(NB):
                    last = v.tensor_tensor(mixw[:, :, :, n * NB + i], src[:, i, :, :],
                                           seqmask.unsqueeze(1).broadcast_to([P, G, NB]), ALU.mult)
                last.then_inc(mix_sb, 1)

            def prepare_qkv():
                for c in range(KC // 2):
                    dve.wait_ge(wqkv_hi_sb, c + 1)
                    minus(wqkv_lo[:, c, 0:D].rearrange("p (g k d) -> p g k d", g=NQ, k=NKV),
                          rawq[:, c, :].rearrange("p (k g d) -> p g k d", k=NKV, g=NQ),
                          wqkv_hi[:, c, 0:D].rearrange("p (g k d) -> p g k d", g=NQ, k=NKV)).then_inc(wqkv_lo_sb, 1)
                dve.wait_ge(wqkv_hi_sb, KC + 1)
                minus(wqkv_lo[:, :, D:D + 2 * P], rawkv, wqkv_hi[:, :, D:D + 2 * P]).then_inc(wqkv_lo_sb, 1)

            def prepare_conv_rows():
                dve.wait_ge(ld["convw"], 16)
                for j in range(NB):
                    for g in range(S // CG):
                        last = v.tensor_copy(cvR[:, :, j, g, :], cvS[:, :].rearrange("o (i k) -> o k i", i=CG))
                last.then_inc(cvR_sb, 1)

            def prepare_conv():
                dve.wait_ge(cv_ps, 1)
                v.tensor_tensor(cvT[:, :, :], ps[:, 7, 0:TAPS * S].rearrange("p (k o) -> p k o", k=TAPS),
                                cst[:, C_CONV:C_CONV + S].unsqueeze(1).broadcast_to([P, TAPS, S]), ALU.mult).then_inc(cv_sb, 1)
                dve.wait_ge(cv_sb, 1)
                dve.wait_ge(pads_sb, 1)
                for j in range(PH):
                    for s in range(SHIFTS):
                        at = TAPS - 1 - (PH * (s - 1) + j + PAD)
                        lo, hi = max(0, -at), min(PH, TAPS - at)
                        v.tensor_copy(convW[S * j:S * (j + 1), s, lo:hi, :], cvT[S * j:S * (j + 1), at + lo:at + hi, :])

            def prepare_base(phases):
                for j in phases:
                    dve.wait_ge(base_hi_sb, j + 1)
                    minus(base_lo[:, j, :], ps[:, 4 + j % 2, :], base_hi[:, j, :]).then_inc(base_lo_sb, 1)

            def prepare_experts():
                dve.wait_ge(ld["emap"], 16)
                v.tensor_copy(emapF[:, :], emapB[:, :]).then_inc(emapF_sb, 1)
                dve.wait_ge(emapF_sb, 1)
                v.tensor_tensor(selE[:, :, :], emapF[:, :].unsqueeze(1).broadcast_to([P, NE, NR]),
                                cst[:, C_E:C_E + NE].unsqueeze(2).broadcast_to([P, NE, NR]), ALU.is_equal).then_inc(emapF_sb, 1)
                dve.wait_ge(emapF_sb, 2)
                v.tensor_scalar(expert[:, :, :], selE[:, :, :], LORA_SCALE, None, ALU.mult).then_inc(emapF_sb, 1)

            def prepare_lora():
                dve.wait_ge(lora_hi_sb, 1)
                minus(lora_lo[:, :], ps[:, 7, :], lora_hi[:, :])

            def prepare_ar():
                for h in range(2):
                    dve.wait_ge(ar_hi_sb, h + 1)
                    last = minus(ar_lo[:, 2 * h:2 * h + 2, 0:P + NR],
                                 ps[:, 4 + h, :].rearrange("p (c n) -> p c n", c=2)[:, :, 0:P + NR],
                                 ar_hi[:, 2 * h:2 * h + 2, 0:P + NR])
                last.then_inc(prep_sb, 1)
                dve.wait_ge(ld["routerbB"], 16)

            def route(u):
                dve.wait_ge(ar_sb, u + 1)
                v.tensor_tensor(lg[:, :], arS[:, P:P + NR], routerbB[:, :], ALU.add).then_inc(lg_sb, 1)
                dve.wait_ge(lg_sb, u + 1)
                v.tensor_reduce(top[:, :], lg[:, :], AX.X, ALU.max).then_inc(top_sb, 1)
                dve.wait_ge(top_sb, u + 1)
                v.tensor_scalar(lgs[:, :], lg[:, :], top[:, :], None, ALU.subtract).then_inc(lgs_sb, 1)

            def route2(u):
                dve.wait_ge(ex_sb, u + 1)
                v.tensor_reduce(exZ[:, :], ex[:, :], AX.X, ALU.add)
                v.max(top2[:, :], ex[:, :]).then_inc(top2_sb, 1)
                dve.wait_ge(top2_sb, u + 1)
                v.reciprocal(exR[:, :], exZ[:, :])
                v.match_replace(out=rest[:, :], in_to_replace=top2[:, :], in_values=ex[:, :], imm_value=0.0).then_inc(rest_sb, 1)
                dve.wait_ge(rest_sb, u + 1)
                v.tensor_tensor(sel[:, :], ex[:, :], rest[:, :], ALU.subtract).then_inc(sel_sb, 1)
                dve.wait_ge(sel_sb, u + 1)
                v.tensor_tensor(selE[:, :, :], sel[:, :].unsqueeze(1).broadcast_to([P, NE, NR]), expert[:, :, :],
                                ALU.mult).then_inc(selE_sb, 1)
                dve.wait_ge(selE_sb, u + 1)
                v.tensor_reduce(we[:, :], selE[:, :, :], AX.X, ALU.add).then_inc(we_sb, 1)
                dve.wait_ge(we_sb, u + 1)
                v.scalar_tensor_tensor(hw[:, :, :], arS[:, 0:P].rearrange("p (e r) -> p e r", e=NE), exR[:, :],
                                       we[:, :].unsqueeze(2).broadcast_to([P, NE, RANK]), ALU.mult, ALU.mult
                                       ).then_inc(hw_sb, 1)

            def rope(t):
                for n, (ready, at, width) in enumerate(((q_ps, 0, D), (qkv_ps, D, P))):
                    dve.wait_ge(ready, t + 1)
                    h = width // HD
                    src, a, b = (w.rearrange("p (h d) -> p h d", d=HD) for w in
                                 (ps[:, n, 0:width], t1[:, at:at + width], t2[:, at:at + width]))
                    v.tensor_tensor(a, src, cst[:, C_COS:C_SIN].unsqueeze(1).broadcast_to([P, h, HD]), ALU.mult)
                    for to, of in ((0, HALF), (HALF, 0)):
                        last = v.tensor_tensor(b[:, :, to:to + HALF], src[:, :, of:of + HALF],
                                               cst[:, C_SIN + to:C_SIN + to + HALF].unsqueeze(1).broadcast_to([P, h, HALF]),
                                               ALU.mult)
                    last.then_inc(rope_t, 1)
                dve.wait_ge(rope_t, 2 * (t + 1))
                v.tensor_tensor(qk[:, :], t1, t2[:, :], ALU.add).then_inc(qk_sb, 1)
                v.tensor_tensor(vm[:, :, :, 0:HD],
                                ps[:, 1, P:2 * P].rearrange("p (k d) -> p k d", d=HD).unsqueeze(2).broadcast_to([P, NKV, NB, HD]),
                                seqmask.unsqueeze(1).unsqueeze(3).broadcast_to([P, NKV, NB, HD]), ALU.mult).then_inc(vm_sb, 1)

            def keys(t):
                dve.wait_ge(qT_ps, t + 1)
                v.tensor_tensor(kT,
                                ps[:, 3, 0:P].rearrange("p (b m) -> p b m", m=S).unsqueeze(2).broadcast_to([P, NB, NKV, S]),
                                kvmask.unsqueeze(1).unsqueeze(3).broadcast_to([P, NB, NKV, S]), ALU.mult).then_inc(kT_sb, 1)

            def softmax(t):
                for h in range(2):
                    dve.wait_ge(s_ps, 2 * t + 1 + h)
                    s3 = ps[:, h, :].rearrange("p (h m) -> p h m", m=S)
                    m = mx[:, 16 * h:16 * h + 16]
                    v.tensor_reduce(m, s3, AX.X, ALU.max).then_inc(mx_sb, 1)
                    dve.wait_ge(mx_sb, 2 * t + 1 + h)
                    v.tensor_tensor(sx[:, D * h:D * h + D].rearrange("p (h m) -> p h m", m=S), s3,
                                    m.unsqueeze(2).broadcast_to([P, 16, S]), ALU.subtract).then_inc(sx_sb, 1)

            def normalize(t):
                o5 = ps[:, 4:6, 0:4 * NB * VW].rearrange("p a (k b c) -> p a k b c", k=4, b=NB)
                for a in range(2):
                    dve.wait_ge(o_ps, 2 * t + 1 + a)
                    v.reciprocal(rz[:, 4 * a:4 * a + 4, :], o5[:, a, :, :, HD]).then_inc(rz_sb, 1)
                    dve.wait_ge(rz_sb, 2 * t + 1 + a)
                    last = v.tensor_tensor(on.rearrange("p b (k d) -> p k b d", d=HD)[:, 4 * a:4 * a + 4, :, :],
                                           o5[:, a, :, :, 0:HD],
                                           rz[:, 4 * a:4 * a + 4, :].unsqueeze(3).broadcast_to([P, 4, NB, HD]), ALU.mult)
                last.then_inc(on_sb, 1)

            def steps(t):
                if live(t - 1):
                    dve.wait_ge(oT_ps, t)
                    dve.wait_ge(oT_hi_sb, t)
                    minus(oT_lo[:, :, :, :], ps[:, 6, :].rearrange("p (b g q) -> p g b q", b=NB, g=NQ),
                          oT_hi[:, :, :, :]).then_inc(oT_lo_sb, 1)
                if live(t - 2):
                    route(t - 2)
                if live(t):
                    rope(t)
                if live(t - 2):
                    route2(t - 2)
                if peeled(t, 0):
                    prepare_conv()
                    prepare_base((0, 1))
                if live(t - 1):
                    dve.wait_ge(wo_ps, t)
                    dve.wait_ge(xr_in, 16 * t)
                    wait(dve, x1b_sb, t - 1)
                    v.tensor_tensor(x1, ps[:, 4, :].rearrange("p (j n) -> p j n", j=PH),
                                    xr[:, :].rearrange("p (n j) -> p j n", j=PH), ALU.add).then_inc(x1_sb, 1)
                if live(t):
                    keys(t)
                if peeled(t, 0):
                    prepare_base((2, 3))
                    prepare_lora()
                if live(t - 1):
                    dve.wait_ge(x1_sb, t)
                    by_phase(v.tensor_copy, (0, 2)).then_inc(ph_dve, 1)
                if live(t - 2):
                    dve.wait_ge(hwT_hi_sb, t - 1)
                    minus(hwT_lo[:, :], ps[:, 7, 0:P], hwT_hi[:, :]).then_inc(hwT_lo_sb, 1)
                if live(t):
                    softmax(t)
                if peeled(t, 0):
                    prepare_ar()
                    prepare_experts()
                if live(t - 2):
                    dve.wait_ge(ffn_ps, t - 1)
                    dve.wait_ge(x1b_sb, t - 1)
                    wait(dve, out_st, 16 * (t - 2))
                    v.tensor_tensor(outS.rearrange("p (n j) -> p j n", j=PH),
                                    ps[:, 6, :].rearrange("p (j n) -> p j n", j=PH), x1b, ALU.add).then_inc(out_sb, 1)
                if peeled(t, 1):
                    dve.wait_ge(convb_in, 16)
                if live(t - 1):
                    dve.wait_ge(z_ps, t)
                    v.tensor_tensor(zs.rearrange("p (j n) -> p j n", j=PH), ps[:, 5, :].rearrange("p (j n) -> p j n", j=PH),
                                    convb[:, bass.ds((t - 1) * P, P)].unsqueeze(1).broadcast_to([P, PH, P]),
                                    ALU.add).then_inc(zs_sb, 1)
                if peeled(t, -1):
                    dve.wait_ge(mixb_in, 16)
                if peeled(t, 0):
                    dve.wait_ge(mixb_in2, 16)
                if live(t + 1):
                    dve.wait_ge(y_ps, t + 2)
                    v.tensor_tensor(ys[:, :].rearrange("p (c n) -> p c n", c=KC), ps[:, 6, :].rearrange("p (c n) -> p c n", c=KC),
                                    mixb[:, bass.ds((t + 1) * P, P)].unsqueeze(1).broadcast_to([P, KC, P]),
                                    ALU.add).then_inc(ys_sb, 1)
                if peeled(t, -1):
                    prepare_qkv()
                    prepare_conv_rows()
                if peeled(t, 0):
                    dve.wait_ge(wo_lo_sb, NQ)
                if live(t):
                    normalize(t)

            iterate(dve, steps)


_INS = ["x", "cond_128", "fside_S_0", "L0_cond_W0", "L0_cond_b0", "L0_cond_W1", "L0_cond_b1", "L0_cond_W2",
        "L0_cond_b2", "L0_cond_weight", "L0_cond_bias_k", "L0_attn_Wq", "L0_attn_Wk", "L0_attn_Wv", "L0_attn_Wo",
        "L0_cond2_weight", "L0_cond2_c_weight", "L0_ffn_base_W", "L0_ffn_base_b", "L0_ffn_router_W",
        "L0_ffn_router_b", "L0_ffn_A", "L0_ffn_B", "L0_ffn_expert_map"]


def kernel(**inputs):
    import concourse.bacc as bacc
    from concourse.bass_utils import run_bass_kernel_spmd

    nc = bacc.Bacc("TRN2", target_bir_lowering=False, num_devices=1)
    arrays, args = {}, []
    for name in _INS:
        arrays[name] = np.ascontiguousarray(inputs[name])
    arrays["const"] = constants()
    for name, a in arrays.items():
        args.append(nc.dram_tensor(name, a.shape, mybir.dt.from_np(a.dtype), kind="ExternalInput").ap())
    out = nc.dram_tensor("out", (B, S, D), F32, kind="ExternalOutput").ap()
    build(nc, *args, out)
    r = run_bass_kernel_spmd(nc, [arrays], core_ids=[0])
    return r.results[0]["out"]
```
